# Optimizing a Trainium2 kernel written in Bass

```python
import numpy as np
import jax
import jax.numpy as jnp

def _softmax(x, axis=-1):
    return jax.nn.softmax(x, axis=axis)

def _gelu(x):
    return jax.nn.gelu(x, approximate=True)

def _silu(x):
    return jax.nn.silu(x)

def _sigmoid(x):
    return jax.nn.sigmoid(x)

def _layernorm(x, axis=-1, eps=1e-05):
    m = jnp.mean(x, axis=axis, keepdims=True)
    v = jnp.var(x, axis=axis, keepdims=True)
    return (x - m) / jnp.sqrt(v + eps)

def _scatter_add(tgt, idx, src, axis=0):
    return tgt.at[idx].add(src)

def _segment_sum(src, seg, n):
    return jax.ops.segment_sum(src, seg, n)
kernel_name = 'mk_adaln_attn_ffn_d1_seqx_r4_40bc87'

def setup_inputs(seed: int=0):
    np.random.seed(seed)
    _w = jnp.asarray

    def _rec_inputs():
        import jax
        import jax.numpy as jnp
        _rk = jax.random.key(seed)
        x = -0.000125 + 0.9999 * jax.random.normal(jax.random.fold_in(_rk, 1), (64, 64, 1024), jnp.float32)
        _lenS = 64 - jax.random.randint(jax.random.fold_in(_rk, 7), (64,), 0, max(1, 64 // 4) + 1, jnp.int32)
        _lenS2 = 64 - jax.random.randint(jax.random.fold_in(_rk, 8), (64,), 0, max(1, 64 // 4) + 1, jnp.int32)
        cond_128 = 0.0061147 + 1.02565 * jax.random.normal(jax.random.fold_in(_rk, 11), (64, 128), jnp.float32)
        fside_S_0 = -0.022604 + 0.987366 * jax.random.normal(jax.random.fold_in(_rk, 12), (64,), jnp.float32)
        return (x, cond_128, fside_S_0)
    x, cond_128, fside_S_0 = _rec_inputs()

    def _L0_cond_setup():
        import jax, jax.numpy as jnp
        import numpy as np
        K = 8
        T = 1.0
        D_EMBD = 128
        IN_C = 64
        OUT_C = 64
        BS = 32
        H = 1024
        HID = 128
        key = jax.random.key(seed)
        ks = jax.random.split(key, 10)
        s = lambda fan_in: 1.0 / np.sqrt(fan_in)
        return {'x': jax.random.normal(ks[0], (BS, IN_C, H), dtype=jnp.float32), 'embedding': jax.random.normal(ks[1], (BS, D_EMBD), dtype=jnp.float32), 'W0': jax.random.normal(ks[2], (D_EMBD, HID), dtype=jnp.float32) * s(D_EMBD), 'b0': jnp.zeros((HID,), dtype=jnp.float32), 'W1': jax.random.normal(ks[3], (HID, HID), dtype=jnp.float32) * s(HID), 'b1': jnp.zeros((HID,), dtype=jnp.float32), 'W2': jax.random.normal(ks[4], (HID, K), dtype=jnp.float32) * s(HID), 'b2': jnp.zeros((K,), dtype=jnp.float32), 'weight': jax.random.normal(ks[5], (K, OUT_C, IN_C, 1), dtype=jnp.float32) * s(IN_C), 'bias_k': jax.random.normal(ks[6], (K, OUT_C), dtype=jnp.float32) * 0.1}
    _L0_cond_all = _L0_cond_setup()
    _L0_cond_in = {k: v for k, v in _L0_cond_all.items() if k in ('W0', 'b0', 'W1', 'b1', 'W2', 'b2', 'weight', 'bias_k')}
    del _L0_cond_all

    def _L0_attn_setup():
        import jax, jax.numpy as jnp
        import numpy as np
        EMB_DIM = 1024
        N_HEADS = 32
        QKV_DIM = EMB_DIM // N_HEADS
        B, S = (4, 1024)
        key = jax.random.key(seed)
        ks = jax.random.split(key, 7)
        std = 1.0 / np.sqrt(EMB_DIM)
        x = jax.random.normal(ks[0], (B, S, EMB_DIM), dtype=jnp.float32)
        Wq = jax.random.normal(ks[1], (EMB_DIM, QKV_DIM, N_HEADS), dtype=jnp.float32) * std
        bq = jnp.zeros((QKV_DIM, N_HEADS), dtype=jnp.float32)
        Wk = jax.random.normal(ks[2], (EMB_DIM, QKV_DIM, 1), dtype=jnp.float32) * std
        bk = jnp.zeros((QKV_DIM, 1), dtype=jnp.float32)
        Wv = jax.random.normal(ks[3], (EMB_DIM, QKV_DIM, 1), dtype=jnp.float32) * std
        bv = jnp.zeros((QKV_DIM, 1), dtype=jnp.float32)
        return {'x': x, 'Wq': Wq, 'bq': bq, 'Wk': Wk, 'bk': bk, 'Wv': Wv, 'bv': bv}
    _L0_attn_all = _L0_attn_setup()
    _L0_attn_in = {k: v for k, v in _L0_attn_all.items() if k in ('Wq', 'bq', 'Wk', 'bk', 'Wv', 'bv')}
    del _L0_attn_all

    def _L0_cond2_setup():
        import jax, jax.numpy as jnp
        import numpy as np
        from jax import lax
        N, C_IN, L = (32, 64, 1024)
        C_OUT, K, GROUPS = (64, 9, 4)
        C_DIM, PAD, STRIDE = (128, 4, 1)
        key = jax.random.key(seed)
        k1, k2, k3, k4, k5 = jax.random.split(key, 5)
        x = jax.random.normal(k1, (N, C_IN, L), dtype=jnp.float32)
        c = jax.random.normal(k2, (N, C_DIM), dtype=jnp.float32)
        weight = jax.random.normal(k3, (C_OUT, C_IN // GROUPS, K), dtype=jnp.float32)
        c_weight = jax.random.normal(k4, (C_OUT, C_DIM), dtype=jnp.float32)
        bias = jax.random.normal(k5, (C_OUT,), dtype=jnp.float32)
        return {'x': x, 'c': c, 'weight': weight, 'c_weight': c_weight, 'bias': bias}
    _L0_cond2_all = _L0_cond2_setup()
    _L0_cond2_in = {k: v for k, v in _L0_cond2_all.items() if k in ('weight', 'c_weight')}
    del _L0_cond2_all

    def _L0_ffn_setup():
        import jax, jax.numpy as jnp
        import numpy as np
        NUM_BITS = 4
        QMAX = 2 ** NUM_BITS - 1
        VALS_PER_BYTE = 8 // NUM_BITS
        OUT_F, IN_F = (1024, 1024)

        def _unpack(packed):
            shifts = jnp.arange(VALS_PER_BYTE, dtype=jnp.uint8) * NUM_BITS
            q = packed[:, None, :] >> shifts[None, :, None] & jnp.uint8(QMAX)
            return q.reshape(-1, packed.shape[-1]).astype(jnp.float32)
        key = jax.random.key(seed)
        kx, kw, kb = jax.random.split(key, 3)
        x = jax.random.normal(kx, (4, 512, IN_F), dtype=jnp.float32)
        w = jax.random.normal(kw, (OUT_F, IN_F), dtype=jnp.float32) * 0.02
        min_val, max_val = (w.min(), w.max())
        scale = (max_val - min_val) / QMAX
        zero_point = jnp.clip(jnp.round(QMAX - max_val / scale), 0, QMAX)
        q = jnp.clip(jnp.round(zero_point + w / scale), 0, QMAX).astype(jnp.uint8)
        q2 = q.reshape(OUT_F // VALS_PER_BYTE, VALS_PER_BYTE, IN_F)
        packed_weight = (q2[:, 0, :] | q2[:, 1, :] << 4).astype(jnp.uint8)
        bias = jax.random.normal(kb, (OUT_F,), dtype=jnp.float32) * 0.01
        return {'x': x, 'packed_weight': packed_weight, 'scale': scale, 'zero_point': zero_point, 'bias': bias}
    _L0_ffn_all = _L0_ffn_setup()
    _L0_ffn_in = {k: v for k, v in _L0_ffn_all.items() if k in ('packed_weight', 'scale', 'zero_point', 'bias')}
    del _L0_ffn_all
    return {'x': x, 'cond_128': cond_128, 'fside_S_0': fside_S_0, 'L0_cond_W0': _L0_cond_in['W0'], 'L0_cond_b0': _L0_cond_in['b0'], 'L0_cond_W1': _L0_cond_in['W1'], 'L0_cond_b1': _L0_cond_in['b1'], 'L0_cond_W2': _L0_cond_in['W2'], 'L0_cond_b2': _L0_cond_in['b2'], 'L0_cond_weight': _L0_cond_in['weight'], 'L0_cond_bias_k': _L0_cond_in['bias_k'], 'L0_attn_Wq': _L0_attn_in['Wq'], 'L0_attn_bq': _L0_attn_in['bq'], 'L0_attn_Wk': _L0_attn_in['Wk'], 'L0_attn_bk': _L0_attn_in['bk'], 'L0_attn_Wv': _L0_attn_in['Wv'], 'L0_attn_bv': _L0_attn_in['bv'], 'L0_cond2_weight': _L0_cond2_in['weight'], 'L0_cond2_c_weight': _L0_cond2_in['c_weight'], 'L0_ffn_packed_weight': _L0_ffn_in['packed_weight'], 'L0_ffn_scale': _L0_ffn_in['scale'], 'L0_ffn_zero_point': _L0_ffn_in['zero_point'], 'L0_ffn_bias': _L0_ffn_in['bias']}

def reference(x, cond_128, fside_S_0, L0_cond_W0, L0_cond_b0, L0_cond_W1, L0_cond_b1, L0_cond_W2, L0_cond_b2, L0_cond_weight, L0_cond_bias_k, L0_attn_Wq, L0_attn_bq, L0_attn_Wk, L0_attn_bk, L0_attn_Wv, L0_attn_bv, L0_cond2_weight, L0_cond2_c_weight, L0_ffn_packed_weight, L0_ffn_scale, L0_ffn_zero_point, L0_ffn_bias):
    import jax
    import jax.numpy as jnp

    def _L0_cond_ref(x, embedding, W0, b0, W1, b1, W2, b2, weight, bias_k):
        import jax, jax.numpy as jnp
        import numpy as np
        K = 8
        T = 1.0
        D_EMBD = 128
        IN_C = 64
        OUT_C = 64
        BS = 32
        H = 1024
        HID = 128
        h = jax.nn.gelu(embedding @ W0 + b0, approximate=False)
        h = jax.nn.gelu(h @ W1 + b1, approximate=False)
        att = jax.nn.softmax((h @ W2 + b2) / T, axis=-1)
        agg_w = jnp.einsum('bk,koi->boi', att, weight[..., 0])
        agg_b = att @ bias_k
        out = jnp.einsum('boi,bih->boh', agg_w, x) + agg_b[:, :, None]
        return out

    def _L0_attn_ref(x, Wq, bq, Wk, bk, Wv, bv):
        import jax, jax.numpy as jnp
        import numpy as np
        EMB_DIM = 1024
        N_HEADS = 32
        QKV_DIM = EMB_DIM // N_HEADS
        B, S = (4, 1024)
        q = jnp.einsum('bsD,Ddh->bsdh', x, Wq) + bq
        k = (jnp.einsum('bsD,Ddh->bsdh', x, Wk) + bk)[..., 0]
        v = (jnp.einsum('bsD,Ddh->bsdh', x, Wv) + bv)[..., 0]
        qkv_dim = q.shape[-2]
        n_heads = q.shape[-1]
        scale = 1.0 / jnp.sqrt(jnp.asarray(qkv_dim, dtype=q.dtype))
        scores = jnp.einsum('bsdh,bse->bsde', q, k) * scale
        p = jax.nn.softmax(scores, axis=-1)
        o = jnp.einsum('bsde,bse->bsd', p, v)
        out = jnp.broadcast_to(o[..., None], o.shape + (n_heads,))
        return out.reshape(x.shape[:-1] + (qkv_dim * n_heads,))

    def _L0_cond2_ref(x, c, weight, c_weight, bias):
        import jax, jax.numpy as jnp
        import numpy as np
        from jax import lax
        N, C_IN, L = (32, 64, 1024)
        C_OUT, K, GROUPS = (64, 9, 4)
        C_DIM, PAD, STRIDE = (128, 4, 1)
        out = lax.conv_general_dilated(x, weight, window_strides=(STRIDE,), padding=[(PAD, PAD)], dimension_numbers=('NCH', 'OIH', 'NCH'), feature_group_count=GROUPS)
        ctx = jnp.einsum('nd,od->no', c, c_weight)
        out = out + ctx[:, :, None] + bias[None, :, None]
        return out

    def _L0_ffn_ref(x, packed_weight, scale, zero_point, bias):
        import jax, jax.numpy as jnp
        import numpy as np
        NUM_BITS = 4
        QMAX = 2 ** NUM_BITS - 1
        VALS_PER_BYTE = 8 // NUM_BITS
        OUT_F, IN_F = (1024, 1024)

        def _unpack(packed):
            shifts = jnp.arange(VALS_PER_BYTE, dtype=jnp.uint8) * NUM_BITS
            q = packed[:, None, :] >> shifts[None, :, None] & jnp.uint8(QMAX)
            return q.reshape(-1, packed.shape[-1]).astype(jnp.float32)
        w = scale * (_unpack(packed_weight) - zero_point)
        return jnp.einsum('bsi,oi->bso', x, w) + bias
    x = x + _L0_attn_ref(_L0_cond_ref(x, cond_128, L0_cond_W0, L0_cond_b0, L0_cond_W1, L0_cond_b1, L0_cond_W2, L0_cond_b2, L0_cond_weight, L0_cond_bias_k), L0_attn_Wq, L0_attn_bq, L0_attn_Wk, L0_attn_bk, L0_attn_Wv, L0_attn_bv)
    x = x + _L0_ffn_ref(_L0_cond2_ref(x, cond_128, L0_cond2_weight, L0_cond2_c_weight, fside_S_0), L0_ffn_packed_weight, L0_ffn_scale, L0_ffn_zero_point, L0_ffn_bias)
    return x

_drawn_inputs = setup_inputs


def setup_inputs(seed=0):
    import zlib

    import numpy as np

    out = dict(_drawn_inputs(seed))
    spreads = {'L0_cond_b0': (0.0, 0.8),
     'L0_cond_b1': (0.0, 0.8),
     'L0_cond_b2': (0.0, 0.8),
     'L0_attn_bq': (0.0, 0.8),
     'L0_attn_bk': (0.0, 0.8),
     'L0_attn_bv': (0.0, 0.8)}
    factors = {'L0_cond_W0': 3.978,
     'L0_cond_W1': 3.582,
     'L0_cond_W2': 3.531,
     'L0_cond_bias_k': 7.821,
     'L0_attn_Wq': 7.233,
     'L0_attn_Wk': 7.362,
     'L0_ffn_bias': 64.0}
    for name, (base, spread) in spreads.items():
        noise = np.random.default_rng([zlib.crc32(name.encode()), seed]).standard_normal(out[name].shape)
        drawn = base * np.exp(spread * noise) if base else spread * noise
        out[name] = jnp.asarray(drawn.astype(out[name].dtype))
    for name, factor in factors.items():
        out[name] = (out[name] * factor).astype(out[name].dtype)
    return out
```

```python
import concourse.bass as bass
from concourse import mybir
from contextlib import ExitStack

F32 = mybir.dt.float32
F32R = mybir.dt.float32r
I32 = mybir.dt.int32
U8 = mybir.dt.uint8
ALU = mybir.AluOpType
ACT = mybir.ActivationFunctionType
AX = mybir.AxisListType

P = 128
B, S, D = 64, 64, 1024
DH, NH = 32, 32
KE = 8
R = D // P
G, CG = 4, 16
TAPS, PAD = 9, 4
UB = 4
TU = 2
UT = UB * S
NU = B // UB
NT = NU * TU
SLOTS = 16
W3 = 3 * DH
COLS = 1 + G * UB * (P + 1)
HALF = D // 2
ZLIM = 1000.0
NX = 5


def block_program(nc, x, cond_t, w0, b0, w1, b1, w2, b2, mix_w, mix_b, wq, bq, wk, bk, wv, bv,
                  conv_w, ctx_w, conv_bias, packed_t, scale, zero_point, ffn_bias, out):
    ctx = ExitStack()
    with ctx:
        def sb(name, shape, dt=F32):
            return ctx.enter_context(nc.sbuf_tensor(name, shape, dt))

        def ps(name):
            return ctx.enter_context(nc.psum_tensor(name, [P, 512], F32))

        def sem(name):
            return ctx.enter_context(nc.semaphore(name))

        x_nat = sb("x_nat", [P, NX, TU, D])
        x_t = sb("x_t", [P, 2, R, UT])
        x1_t = sb("x1_t", [P, UT // CG, R, CG])
        w3 = sb("w3", [P, R, W3])
        z_sb = sb("z_sb", [P, TU, W3])
        qkv_bias = sb("qkv_bias", [P, TU, W3])
        qkv = sb("qkv", [P, TU, W3])
        prob = sb("prob", [P, TU, DH, DH])
        k_max = sb("k_max", [P, TU])
        k_min = sb("k_min", [P, TU])
        top = sb("top", [P, TU, DH])
        top2 = sb("top2", [P, TU, DH])
        den = sb("den", [P, TU, DH])
        rden = sb("rden", [P, TU, DH])
        num = sb("num", [P, TU, DH])
        o_rep = sb("o_rep", [P, TU, DH, 4])
        o_t = sb("o_t", [P, UT])
        c_hi = sb("c_hi", [P, COLS], F32R)
        c_lo = sb("c_lo", [P, COLS], F32R)
        y_hi = sb("y_hi", [P, COLS], F32R)
        y_lo = sb("y_lo", [P, COLS], F32R)
        u_sb = sb("u_sb", [P, 2, UB * P])
        u_hi = sb("u_hi", [P, 2, R, UT], F32R)
        u_lo = sb("u_lo", [P, 2, R, UT], F32R)
        w_ffn = sb("w_ffn", [P, R, D], F32R)
        cw_hi = sb("cw_hi", [P, 2, G, P], F32R)
        cw_lo = sb("cw_lo", [P, 2, G, P], F32R)
        mix_t = sb("mix_t", [P, NT, S])
        ffn_b = sb("ffn_b", [P, D])
        rest_hi = sb("rest_hi", [P, P], F32R)
        rest_lo = sb("rest_lo", [P, P], F32R)
        ident = sb("ident", [P, P])
        ones = sb("ones", [P, P])
        cond_sb = sb("cond_sb", [P, B])
        w0_sb = sb("w0_sb", [P, P])
        w1_sb = sb("w1_sb", [P, P])
        w2_sb = sb("w2_sb", [P, KE])
        b01_sb = sb("b01_sb", [P, 2])
        b2_sb = sb("b2_sb", [B, KE])
        h_sb = sb("h_sb", [P, 2, B])
        att = sb("att", [B, 4, KE])
        att_s = sb("att_s", [B, 4])
        att_t = sb("att_t", [KE, B])
        mixb_sb = sb("mixb_sb", [KE, P])
        mix_bias = sb("mix_bias", [P, NT])
        cbias_sb = sb("cbias_sb", [P, G])
        u_bias = sb("u_bias", [P, G, B])
        sc = sb("sc", [P, 1])
        zp = sb("zp", [P, 5])
        zi = sb("zi", [P, 1], I32)
        flag = sb("flag", [1, 2], I32)
        bias3 = sb("bias3", [P, W3])
        col3 = sb("col3", [P, W3])
        cw = u_sb[:, :, :].rearrange("p y (g n) -> p y g n", g=G)
        spare = x1_t[:, :, :, :].rearrange("p b r c -> p (b r c)")
        mixw_lo = spare[0:KE, :]
        mixw_hi = x_t[0:KE, 1, :, :].rearrange("k r t -> k (r t)")
        mixed_lo = prob[0:B, :, :, :].rearrange("b t d e -> b (t d e)")
        mixed_hi = spare[0:B, :]
        packed = spare[:, 0:1024].bitcast(U8).rearrange("p (r n) -> p r n", n=HALF)
        low4 = spare[:, 1024:2048].bitcast(U8).rearrange("p (r n) -> p r n", n=HALF)
        ctx_sb = (o_rep[:, :, :, :].rearrange("p t d e -> p t (d e)"),
                  o_t[:, :].rearrange("p (t n) -> p t n", t=2))
        bq_tmp = ffn_b[:, :].rearrange("p (d h) -> p d h", h=NH)

        p_xt, p_z, p_sm, p_x2, p_conv, p_ut = (ps(n) for n in ("p_xt", "p_z", "p_sm", "p_x2", "p_conv", "p_ut"))
        p_f = [ps("p_f0"), ps("p_f1")]

        mixed_dram = nc.dram_tensor("mixed_dram", [B, S * S], F32).ap()

        s_small = sem("s_small")
        s_small2 = sem("s_small2")
        s_wq = [sem(f"s_wq{i}") for i in range(4)]
        s_wkv = sem("s_wkv")
        s_mw = sem("s_mw")
        s_pk = sem("s_pk")
        s_cw = sem("s_cw")
        s_x = [sem(f"s_xload{i}") for i in range(NX)]
        s_out = [sem(f"s_out{i}") for i in range(NX)]
        s_yd = [sem(f"s_yd{g}") for g in range(G)]
        s_pool0 = sem("s_pool0")
        s_pe0 = sem("s_pe0")
        s_act0 = sem("s_act0")
        s_dve0 = sem("s_dve0")
        s_mixed = sem("s_mixed")
        s_mixedc = sem("s_mixedc")
        s_mixedd = sem("s_mixedd")
        s_mixt = sem("s_mixt")
        s_bq = sem("s_bq")
        s_bqr = sem("s_bqr")
        s_ffb = sem("s_ffb")
        s_w3 = sem("s_w3")
        s_wf = sem("s_wf")
        s_xt = sem("s_xt")
        s_xtc = sem("s_xtc")
        s_z = sem("s_z")
        s_zc = sem("s_zc")
        s_mix = sem("s_mix")
        s_qb = sem("s_qb")
        s_qkv = sem("s_qkv")
        s_top = sem("s_top")
        s_sub = sem("s_sub")
        s_exp = sem("s_exp")
        s_sm = sem("s_sm")
        s_ot = sem("s_ot")
        s_otc = sem("s_otc")
        s_x1t = sem("s_x1t")
        s_xb = sem("s_xb")
        s_x1 = sem("s_x1")
        s_x2 = sem("s_x2")
        s_x2h = sem("s_x2h")
        s_x2l = sem("s_x2l")
        s_conv = sem("s_conv")
        s_u = sem("s_u")
        s_ut = sem("s_ut")
        s_uth = sem("s_uth")
        s_utl = sem("s_utl")
        s_f = sem("s_f")
        s_res = sem("s_res")

        block = ctx.enter_context(nc.Block())

        def xbuf(u):
            return x_nat[:, u % NX, :, :]

        def col(g, n):
            return 1 + (g * UB + n) * (P + 1)

        def runs(t, g):
            return t[:, col(g, 0):col(g, 0) + UB * (P + 1)].rearrange("p (n c) -> p n c", c=P + 1)[:, :, 0:P]

        def ut_view(t, u, g):
            v = t[:, u % 2, :, :].rearrange("p r (n c) -> p n r c", n=UB)
            return v[:, :, :, g * CG:(g + 1) * CG]

        N_SMALL, N_SMALL2 = 9, 7
        N_CW = 2 * R
        NI = NU + 4

        @block.sync
        def _(eng):
            def load_x(u):
                if u >= NX:
                    eng.wait_ge(s_out[u % NX], 32 * (u // NX))
                for t in range(TU):
                    row = (u * TU + t) * P
                    eng.dma_start(x_nat[:, u % NX, t, :], x[row:row + P, :]).then_inc(s_x[u % NX], 16)

            def store(d, t):
                eng.wait_ge(s_res, 4 * d + 2 * t + 2)
                row = (d * TU + t) * P
                eng.dma_start(out[row:row + P, :], x_nat[:, d % NX, t, :]).then_inc(s_out[d % NX], 16)

            load_x(0)
            for c in range(4):
                eng.dma_start(x_nat[:, 1 + c, :, :], wq[:, 2 * c:2 * c + 2, :]).then_inc(s_wq[c], 16)
            for t in range(2):
                eng.dma_start(w3[:, :, DH * (1 + t):DH * (2 + t)], (wk, wv)[t]).then_inc(s_wkv, 16)
            for j, src in enumerate((mixed_lo, mixed_hi)):
                eng.wait_ge(s_mixedc, 4 * (j + 1))
                eng.dma_start(mixed_dram[:, 2048 * j:2048 * j + 2048], src).then_inc(s_mixedd, 16)
            eng.wait_ge(s_mixedd, 32)
            for h in range(2):
                eng.dma_start(mix_t[h * S:h * S + S, :, :],
                              mixed_dram.rearrange("(t h) (i s) -> h i t s", h=2, i=S)[h]).then_inc(s_mixt, 16)
            eng.dma_start(packed, packed_t).then_inc(s_pk, 16)
            eng.wait_ge(s_bqr, 1)
            eng.dma_start(ffn_b[:, :], ffn_bias.broadcast_to([P, D])).then_inc(s_ffb, 16)

            for i in range(NI):
                a, b, d = i, i - 1, i - 3
                for slot in range(SLOTS):
                    if slot == 2 and 0 <= d - 1 < NU:
                        store(d - 1, 1)
                    if slot == 3 and a + 1 < NU:
                        if 1 <= a + 1 < NX:
                            eng.wait_ge(s_w3, a + 1)
                        load_x(a + 1)
                    if 0 <= b < NU and slot in (7, 9, 11, 13):
                        g = (slot - 7) // 2
                        eng.wait_ge(s_x2h, G * b + g + 1)
                        eng.wait_ge(s_x2l, G * b + g + 1)
                        if b:
                            eng.wait_ge(s_conv, G * (b - 1) + g + 1)
                        c0, n = col(g, 0), UB * (P + 1) - 1
                        for src, dst in ((c_hi[:, :].bitcast(F32), y_hi[:, :].bitcast(F32)), (c_lo[:, :].bitcast(F32), y_lo[:, :].bitcast(F32))):
                            eng.dma_start(dst[0:64, c0:c0 + n], src[0:64, c0 + 1:c0 + 1 + n]).then_inc(s_yd[g], 16)
                            eng.dma_start(dst[64:P, c0:c0 + n], src[64:P, c0 - 1:c0 - 1 + n]).then_inc(s_yd[g], 16)
                    if 0 <= d < NU and slot == 9:
                        store(d, 0)
            for k in range(NX):
                eng.wait_ge(s_out[k], 32 * len(range(k, NU, NX)))

        @block.gpsimd
        def _(eng):
            eng.memset(ident[:, :], 0.0).then_inc(s_pool0, 1)
            eng.memset(u_sb[:, :, :], 0.0).then_inc(s_pool0, 1)
            eng.memset(ones[:, :], 1.0).then_inc(s_pool0, 1)
            eng.wait_ge(s_pool0, 3)
            eng.affine_select(out=ident[:, :], in_=ident[:, :], compare_op=ALU.not_equal, fill=1.0,
                              base=0, pattern=[[-1, P]], channel_multiplier=1).then_inc(s_pool0, 1)
            for t in (c_hi, c_lo, y_hi, y_lo):
                eng.memset(t[:, 0:COLS:P + 1].bitcast(F32), 0.0).then_inc(s_pool0, 1)
            for r in range(R):
                lo, hi = max(0, r - PAD), min(R - 1, r + PAD)
                eng.dma_start(cw[r * CG:(r + 1) * CG, 0, :, lo * CG:(hi + 1) * CG],
                              conv_w[:, :, (lo - r + PAD) * CG:(hi - r + PAD + 1) * CG]).then_inc(s_cw, 16)
                lo, hi, k = (r + PAD, R - 1, 0) if r < PAD else (0, r - PAD, 12 - r)
                eng.dma_start(cw[r * CG:(r + 1) * CG, 1, :, lo * CG:(hi + 1) * CG],
                              conv_w[:, :, k * CG:(k + hi - lo + 1) * CG]).then_inc(s_cw, 16)

            for i in range(NI):
                a, b = i, i - 1
                for slot in range(SLOTS):
                    if 0 <= b < NU and slot == 4:
                        eng.wait_ge(s_otc, b + 1)
                        if b:
                            eng.wait_ge(s_x2, G * b)
                        else:
                            eng.wait_ge(s_wf, 2)
                        eng.tensor_tensor(x1_t[:, :, :, :].rearrange("p b r c -> p r b c"),
                                          x_t[:, b % 2, :, :].rearrange("p r (b c) -> p r b c", c=CG),
                                          o_t[:, :].rearrange("p (b c) -> p b c", c=CG).unsqueeze(1).broadcast_to([P, R, UT // CG, CG]),
                                          ALU.add).then_inc(s_x1t, 1)
                    if 0 <= b < NU and slot == 7:
                        eng.wait_ge(s_xb, b + 1)
                        eng.wait_ge(s_sm, 5 * b + 5)
                        xv = xbuf(b).rearrange("p t (d h) -> p t d h", h=NH)
                        eng.tensor_tensor(xv, xv, o_rep[:, :, :, 0:1].broadcast_to([P, TU, DH, NH]), ALU.add).then_inc(s_x1, 1)
                    if a < NU and slot == 10:
                        eng.wait_ge(s_top, 6 * a + 6)
                        eng.tensor_tensor(prob[:, :, :, :], prob[:, :, :, :],
                                          top[:, :, :].unsqueeze(3).broadcast_to([P, TU, DH, DH]), ALU.subtract).then_inc(s_sub, 1)
                    if a < NU and slot == 13:
                        if a == 0:
                            eng.wait_ge(s_ffb, 16)
                        eng.wait_ge(s_xt, 4 * (a + 1))
                        eng.tensor_tensor(xbuf(a), xbuf(a), ffn_b[:, :].unsqueeze(1).broadcast_to([P, TU, D]), ALU.add).then_inc(s_xb, 1)

        @block.scalar
        def _(eng):
            for dst, src in ((cond_sb, cond_t), (w0_sb, w0), (w1_sb, w1), (w2_sb, w2)):
                eng.dma_start(dst[:, :], src).then_inc(s_small, 16)
            eng.dma_start(b01_sb[:, 0:1], b0).then_inc(s_small, 16)
            eng.dma_start(b01_sb[:, 1:2], b1).then_inc(s_small, 16)
            eng.dma_start(b2_sb[:, :], b2.broadcast_to([B, KE])).then_inc(s_small, 16)
            eng.dma_start(mixb_sb[:, 0:S], mix_b).then_inc(s_small, 16)
            eng.dma_start(mixb_sb[:, S:P], mix_b).then_inc(s_small, 16)
            eng.dma_start(mixw_lo, mix_w[:, 0:2048]).then_inc(s_mw, 16)
            eng.dma_start(mixw_hi, mix_w[:, 2048:4096]).then_inc(s_mw, 16)
            eng.dma_start(bq_tmp, bq.broadcast_to([P, DH * NH]).rearrange("p (d h) -> p d h", h=NH)).then_inc(s_bq, 16)
            eng.dma_start(sc[:, :], scale.broadcast_to([P, 1])).then_inc(s_small2, 16)
            eng.dma_start(zp[:, 0:1], zero_point.broadcast_to([P, 1])).then_inc(s_small2, 16)
            eng.dma_start(cbias_sb[:, :], conv_bias).then_inc(s_small2, 16)
            for n in range(2):
                eng.dma_start(ctx_sb[n], ctx_w[:, 2 * n:2 * n + 2, :]).then_inc(s_small2, 16)
            eng.dma_start(bias3[:, DH:2 * DH], bk.broadcast_to([P, DH])).then_inc(s_small2, 16)
            eng.dma_start(bias3[:, 2 * DH:], bv.broadcast_to([P, DH])).then_inc(s_small2, 16)
            for n, bias in enumerate((b01_sb[:, 0:1], b01_sb[:, 1:2])):
                eng.wait_ge(s_pe0, n + 1)
                eng.activation(h_sb[:, n, :], p_sm[:, 64 * n:64 * n + 64], ACT.Gelu, bias=bias).then_inc(s_act0, 1)
            eng.wait_ge(s_dve0, 3)
            eng.activation(att[:, 1, :], att[:, 0, :], ACT.Exp, accum_out=att_s[:, 2:3]).then_inc(s_act0, 1)
            for c in range(8):
                eng.wait_ge(s_mixed, c + 1)
                dst = (mixed_lo, mixed_hi)[c // 4]
                eng.activation(dst[:, 512 * (c % 4):512 * (c % 4) + 512], p_f[c % 2][0:B, :], ACT.Copy).then_inc(s_mixedc, 1)

            def xt_copy(a, k):
                eng.wait_ge(s_xt, 4 * a + k + 1)
                if a >= 2 and k == 0:
                    eng.wait_ge(s_x1t, a - 1)
                t, r0 = k // 2, 4 * (k % 2)
                eng.activation(x_t[:, a % 2, r0:r0 + 4, t * P:(t + 1) * P],
                               p_xt[:, :].rearrange("p (r t) -> p r t", t=P), ACT.Copy).then_inc(s_xtc, 1)

            def z_copy(a, t):
                eng.wait_ge(s_z, TU * a + t + 1)
                if a:
                    eng.wait_ge(s_mix, TU * (a - 1) + t + 1)
                eng.activation(z_sb[:, t, :], p_z[:, 0:W3], ACT.Copy).then_inc(s_zc, 1)

            def o_copy(b):
                eng.wait_ge(s_ot, b + 1)
                if b:
                    eng.wait_ge(s_x1t, b)
                eng.activation(o_t[:, :], p_sm[:, 192:192 + UT], ACT.Copy).then_inc(s_otc, 1)

            def x2_hi(b, g):
                eng.wait_ge(s_x2, G * b + g + 1)
                if b:
                    eng.wait_ge(s_conv, G * (b - 1) + g + 1)
                eng.activation(runs(c_hi, g), p_x2[:, :].rearrange("p (n c) -> p n c", n=UB), ACT.Copy).then_inc(s_x2h, 1)

            def ut_hi(c, g):
                eng.wait_ge(s_ut, G * c + g + 1)
                if c >= 2:
                    eng.wait_ge(s_f, 4 * (c - 1))
                eng.activation(ut_view(u_hi, c, g),
                               p_ut[:, :].rearrange("p (n r c) -> p n r c", n=UB, r=R), ACT.Copy).then_inc(s_uth, 1)

            for i in range(NI):
                a, b, c = i, i - 1, i - 2
                for slot in range(SLOTS):
                    if a < NU and slot < 4:
                        xt_copy(a, slot)
                    if a < NU and slot in (3, 5):
                        z_copy(a, (slot - 3) // 2)
                    if 0 <= b < NU and slot == 3:
                        o_copy(b)
                    if 0 <= b < NU and slot in (7, 9, 11, 13):
                        x2_hi(b, (slot - 7) // 2)
                    if 0 <= c < NU and slot in (2, 6, 10, 14):
                        ut_hi(c, slot // 4)
                    if a < NU and slot == 12:
                        eng.wait_ge(s_sub, a + 1)
                        flat = prob[:, :, :, :].rearrange("p t d e -> p (t d e)")
                        eng.activation(flat, flat, ACT.Exp, scale=float(DH) ** -0.5).then_inc(s_exp, 1)
                if i == 0:
                    for half, src in enumerate((low4, packed)):
                        eng.wait_ge(s_dve0, 19 + half)
                        eng.activation(w_ffn[:, :, half:D:2], src, ACT.Identity, bias=zp[:, 4:5]).then_inc(s_wf, 1)

        @block.vector
        def _(eng):
            def chunk_sum(c):
                eng.wait_ge(s_wq[c], 16)
                eng.tensor_reduce(w3[:, 2 * c:2 * c + 2, 0:DH],
                                  x_nat[:, 1 + c, :, :].rearrange("p t (d h) -> p t d h", h=NH), AX.X, ALU.add).then_inc(s_w3, 1)

            eng.wait_ge(s_small, 16 * N_SMALL)
            eng.wait_ge(s_pe0, 3)
            eng.tensor_tensor(att[:, 0, :], p_sm[0:B, 128:128 + KE], b2_sb[:, :], ALU.add).then_inc(s_dve0, 1)
            eng.wait_ge(s_dve0, 1)
            eng.tensor_reduce(att_s[:, 0:1], att[:, 0, :], AX.X, ALU.max).then_inc(s_dve0, 1)
            eng.wait_ge(s_dve0, 2)
            eng.tensor_scalar(att[:, 0, :], att[:, 0, :], att_s[:, 0:1], None, ALU.subtract).then_inc(s_dve0, 1)
            eng.wait_ge(s_act0, 3)
            eng.reciprocal(att_s[:, 3:4], att_s[:, 2:3]).then_inc(s_dve0, 1)
            eng.wait_ge(s_dve0, 4)
            eng.tensor_scalar(att[:, 2, :], att[:, 1, :], att_s[:, 3:4], None, ALU.mult).then_inc(s_dve0, 1)
            eng.wait_ge(s_pe0, 4)
            eng.tensor_copy(att_t[:, :], p_sm[0:KE, 192:192 + B]).then_inc(s_dve0, 1)
            eng.wait_ge(s_pe0, 5)
            for h in range(2):
                eng.tensor_copy(mix_bias[h * S:h * S + S, :], p_sm[h * S:h * S + S, 256 + h:256 + B:2]).then_inc(s_dve0, 1)
            eng.wait_ge(s_small2, 16 * N_SMALL2)
            eng.tensor_scalar(zp[:, 1:2], zp[:, 0:1], ZLIM, -ZLIM, ALU.min, ALU.max).then_inc(s_dve0, 1)
            eng.wait_ge(s_dve0, 9)
            eng.tensor_copy(zi[:, :], zp[:, 1:2]).then_inc(s_dve0, 1)
            eng.wait_ge(s_dve0, 10)
            eng.tensor_copy(zp[:, 2:3], zi[:, :]).then_inc(s_dve0, 1)
            eng.wait_ge(s_dve0, 11)
            eng.tensor_tensor(zp[:, 3:4], zp[:, 2:3], zp[:, 0:1], ALU.subtract).then_inc(s_dve0, 1)
            eng.tensor_scalar(zp[:, 4:5], zp[:, 2:3], -1.0, None, ALU.mult).then_inc(s_dve0, 1)
            eng.wait_ge(s_dve0, 13)
            rest = zp[:, 3:4].broadcast_to([P, P])
            eng.tensor_scalar(flag[0:1, 0:1], zp[0:1, 3:4], 0.0, None, ALU.not_equal).then_inc(s_dve0, 1)
            eng.tensor_copy(rest_hi[:, :], rest).then_inc(s_dve0, 1)
            eng.wait_ge(s_dve0, 15)
            eng.tensor_tensor(rest_lo[:, :], rest, rest_hi[:, :].bitcast(F32), ALU.subtract).then_inc(s_dve0, 1)
            eng.wait_ge(s_pe0, 6)
            for g in range(G):
                ins = eng.tensor_scalar(u_bias[:, g, :], p_conv[:, B * g:B * g + B], cbias_sb[:, g:g + 1], sc[:, 0:1], ALU.add, ALU.mult)
            ins.then_inc(s_dve0, 1)
            eng.wait_ge(s_bq, 16)
            eng.tensor_reduce(bias3[:, 0:DH], bq_tmp, AX.X, ALU.add).then_inc(s_bqr, 1)
            for c in range(4):
                chunk_sum(c)
            eng.wait_ge(s_pe0, 7)
            eng.tensor_copy(col3[:, :], p_sm[:, 320:320 + W3]).then_inc(s_dve0, 1)
            eng.wait_ge(s_pk, 16)
            eng.tensor_scalar(low4, packed, 15, None, ALU.bitwise_and).then_inc(s_dve0, 1)
            eng.wait_ge(s_dve0, 19)
            eng.tensor_scalar(packed, packed, 4, None, ALU.logical_shift_right).then_inc(s_dve0, 1)
            eng.wait_ge(s_cw, 16 * N_CW)
            eng.tensor_copy(cw_hi[:, :, :, :], cw).then_inc(s_dve0, 1)
            eng.wait_ge(s_dve0, 21)
            eng.tensor_tensor(cw_lo[:, :, :, :], cw, cw_hi[:, :, :, :].bitcast(F32), ALU.subtract).then_inc(s_dve0, 1)

            def softmax_top(a):
                q = qkv[:, :, 0:DH]
                k = qkv[:, :, DH:2 * DH]

                def wide(x1):
                    return x1[:, :].unsqueeze(2).broadcast_to([P, TU, DH])

                for n, (dst, op) in enumerate(((k_max, ALU.max), (k_min, ALU.min))):
                    if n == 0:
                        eng.wait_ge(s_qkv, a + 1)
                    eng.tensor_reduce(dst[:, :], k, AX.X, op).then_inc(s_top, 1)
                for n, (dst, src) in enumerate(((top, k_max), (top2, k_min))):
                    eng.wait_ge(s_top, 6 * a + n + 1)
                    if n == 0 and a:
                        eng.wait_ge(s_sub, a)
                    eng.tensor_tensor(dst[:, :, :], q, wide(src), ALU.mult).then_inc(s_top, 1)
                eng.wait_ge(s_top, 6 * a + 4)
                eng.tensor_tensor(top[:, :, :], top[:, :, :], top2[:, :, :], ALU.max).then_inc(s_top, 1)
                eng.tensor_tensor(prob[:, :, :, :], q.unsqueeze(3).broadcast_to([P, TU, DH, DH]),
                                  k.unsqueeze(2).broadcast_to([P, TU, DH, DH]), ALU.mult).then_inc(s_top, 1)

            def softmax_sums(a):
                v = qkv[:, :, 2 * DH:]
                eng.wait_ge(s_exp, a + 1)
                eng.tensor_reduce(den[:, :, :], prob[:, :, :, :], AX.X, ALU.add).then_inc(s_sm, 1)
                eng.wait_ge(s_sm, 5 * a + 1)
                eng.tensor_tensor(prob[:, :, :, :], prob[:, :, :, :],
                                  v.unsqueeze(2).broadcast_to([P, TU, DH, DH]), ALU.mult).then_inc(s_sm, 1)

            def softmax_out(b):
                eng.wait_ge(s_sm, 5 * b + 2)
                eng.tensor_reduce(num[:, :, :], prob[:, :, :, :], AX.X, ALU.add).then_inc(s_sm, 1)
                eng.reciprocal(rden[:, :, :], den[:, :, :]).then_inc(s_sm, 1)
                eng.wait_ge(s_sm, 5 * b + 4)
                if b:
                    eng.wait_ge(s_ot, b)
                    eng.wait_ge(s_x1, b)
                eng.tensor_tensor(o_rep[:, :, :, :], num[:, :, :].unsqueeze(3).broadcast_to([P, TU, DH, 4]),
                                  rden[:, :, :].unsqueeze(3).broadcast_to([P, TU, DH, 4]), ALU.mult).then_inc(s_sm, 1)

            def finish(d, f):
                t, j = f // 2, f % 2
                eng.wait_ge(s_f, 4 * d + f + 1)
                if f == 0:
                    eng.wait_ge(s_x1, d + 1)
                part = x_nat[:, d % NX, t, j * HALF:(j + 1) * HALF]
                eng.tensor_tensor(part, p_f[f % 2][:, :], part, ALU.add).then_inc(s_res, 1)

            for i in range(NI):
                a, b, c, d = i, i - 1, i - 2, i - 3
                for slot in range(SLOTS):
                    if slot == 0 and 0 <= d - 1 < NU:
                        finish(d - 1, 3)
                    if slot in (4, 8, 12) and 0 <= d < NU:
                        finish(d, slot // 4 - 1)
                    if 0 <= b < NU and slot == 0:
                        softmax_out(b)
                    if 0 <= c < NU and slot % 4 == 0:
                        g = slot // 4
                        eng.wait_ge(s_conv, G * c + g + 1)
                        if c or g >= 2:
                            eng.wait_ge(s_ut, G * c + g - 1)
                        eng.scalar_tensor_tensor(out=u_sb[:, g % 2, :].rearrange("p (n c) -> p n c", n=UB),
                                                 in0=p_conv[:, :].rearrange("p (n c) -> p n c", n=UB), scalar=sc[:, 0:1],
                                                 in1=u_bias[:, g, UB * c:UB * c + UB].unsqueeze(2).broadcast_to([P, UB, P]),
                                                 op0=ALU.mult, op1=ALU.add).then_inc(s_u, 1)
                    if 0 <= c < NU and slot in (2, 6, 10, 14):
                        g = slot // 4
                        eng.wait_ge(s_uth, G * c + g + 1)
                        eng.tensor_tensor(ut_view(u_lo, c, g), p_ut[:, :].rearrange("p (n r c) -> p n r c", n=UB, r=R),
                                          ut_view(u_hi, c, g).bitcast(F32), ALU.subtract).then_inc(s_utl, 1)
                    if a < NU and slot == 7:
                        for t in range(TU):
                            eng.scalar_tensor_tensor(out=qkv_bias[:, t, :], in0=col3[:, :], scalar=mix_bias[:, TU * a + t:TU * a + t + 1],
                                                     in1=bias3[:, :], op0=ALU.mult, op1=ALU.add).then_inc(s_qb, 1)
                        eng.wait_ge(s_qb, TU * (a + 1))
                        eng.wait_ge(s_mix, TU * (a + 1))
                        eng.tensor_tensor(qkv[:, :, :], p_sm[:, 0:TU * W3].rearrange("p (t w) -> p t w", t=TU),
                                          qkv_bias[:, :, :], ALU.add).then_inc(s_qkv, 1)
                    if 0 <= b < NU and slot in (7, 9, 11, 13):
                        g = (slot - 7) // 2
                        eng.wait_ge(s_x2h, G * b + g + 1)
                        eng.tensor_tensor(runs(c_lo, g), p_x2[:, :].rearrange("p (n c) -> p n c", n=UB),
                                          runs(c_hi, g).bitcast(F32), ALU.subtract).then_inc(s_x2l, 1)
                    if a < NU and slot == 8:
                        softmax_top(a)
                    if a < NU and slot == 14:
                        softmax_sums(a)

        @block.tensor
        def _(eng):
            mm = eng.matmul
            eng.wait_ge(s_small, 16 * N_SMALL)
            mm(p_sm[:, 0:B], w0_sb[:, :], cond_sb[:, :], start=True, stop=True).then_inc(s_pe0, 1)
            eng.wait_ge(s_act0, 1)
            mm(p_sm[:, B:2 * B], w1_sb[:, :], h_sb[:, 0, :], start=True, stop=True).then_inc(s_pe0, 1)
            eng.wait_ge(s_act0, 2)
            mm(p_sm[0:B, 128:128 + KE], h_sb[:, 1, :], w2_sb[:, :], start=True, stop=True).then_inc(s_pe0, 1)
            eng.wait_ge(s_dve0, 5)
            eng.wait_ge(s_pool0, 4)
            eng.transpose(p_sm[0:KE, 192:192 + B], att[:, 2, :], ident[0:B, 0:B]).then_inc(s_pe0, 1)
            eng.wait_ge(s_dve0, 6)
            mm(p_sm[:, 256:256 + B], mixb_sb[:, :], att_t[:, :], start=True, stop=True).then_inc(s_pe0, 1)
            eng.wait_ge(s_mw, 32)
            for c in range(8):
                if c >= 2:
                    eng.wait_ge(s_mixedc, c - 1)
                src = (mixw_lo, mixw_hi)[c // 4]
                mm(p_f[c % 2][0:B, :], att_t[:, :], src[:, 512 * (c % 4):512 * (c % 4) + 512],
                   start=True, stop=True).then_inc(s_mixed, 1)
            eng.wait_ge(s_small2, 16 * N_SMALL2)
            for g in range(G):
                last = mm(p_conv[:, B * g:B * g + B], ctx_sb[g // 2][:, g % 2, :], cond_sb[:, :], start=True, stop=True)
            last.then_inc(s_pe0, 1)
            eng.wait_ge(s_dve0, 14)
            inexact = eng.value_load(flag[0:1, 0:1], min_val=0, max_val=1)

            def transpose_x(a, k):
                if k == 0:
                    eng.wait_ge(s_x[a % NX], 32 * (a // NX + 1))
                if a or k:
                    eng.wait_ge(s_xtc, 4 * a + k)
                t, r0 = k // 2, 4 * (k % 2)
                for r in range(4):
                    last = eng.transpose(p_xt[:, r * P:(r + 1) * P], x_nat[:, a % NX, t, r0 + r:D:R], ident[:, :])
                last.then_inc(s_xt, 1)

            def project(a, t):
                if a == 0 and t == 0:
                    eng.wait_ge(s_w3, 4)
                    eng.wait_ge(s_wkv, 32)
                    eng.wait_ge(s_dve0, 8)
                    for r in range(R):
                        last = mm(p_sm[:, 320:320 + W3], ones[:, :], w3[:, r, :], start=(r == 0), stop=(r == R - 1))
                    last.then_inc(s_pe0, 1)
                eng.wait_ge(s_xtc, 4 * a + 2 * t + 2)
                if a or t:
                    eng.wait_ge(s_zc, TU * a + t)
                for r in range(R):
                    last = mm(p_z[:, 0:W3], x_t[:, a % 2, r, t * P:(t + 1) * P], w3[:, r, :], start=(r == 0), stop=(r == R - 1))
                last.then_inc(s_z, 1)

            def mix(a, t):
                if t == 0:
                    if a == 0:
                        eng.wait_ge(s_mixt, 32)
                        eng.wait_ge(s_dve0, 18)
                    else:
                        eng.wait_ge(s_qkv, a)
                        eng.wait_ge(s_otc, a)
                eng.wait_ge(s_zc, TU * a + t + 1)
                for h in range(2):
                    rows = slice(h * S, h * S + S)
                    last = mm(p_sm[rows, W3 * t:W3 * t + W3], mix_t[rows, TU * a + t, :], z_sb[rows, t, :], start=True, stop=True)
                last.then_inc(s_mix, 1)

            def transpose_o(b):
                eng.wait_ge(s_sm, 5 * b + 5)
                eng.wait_ge(s_qkv, b + 1)
                for t in range(TU):
                    last = eng.transpose(p_sm[:, 192 + t * P:192 + (t + 1) * P],
                                         o_rep[:, t, :, :].rearrange("p d e -> p (d e)"), ident[:, :])
                last.then_inc(s_ot, 1)

            def transpose_x1(b, g):
                if g == 0:
                    eng.wait_ge(s_x1t, b + 1)
                if b or g:
                    eng.wait_ge(s_x2l, G * b + g)
                for n in range(UB):
                    last = eng.transpose(p_x2[:, n * P:(n + 1) * P],
                                         x1_t[:, n * G + g, :, :].rearrange("p r c -> p (r c)"), ident[:, :])
                last.then_inc(s_x2, 1)

            def conv(c, g):
                if c == 0 and g == 0:
                    eng.wait_ge(s_dve0, 22)
                if c or g:
                    eng.wait_ge(s_u, G * c + g)
                eng.wait_ge(s_x2l, G * c + g + 1)
                n = 0
                for k, (hi, lo) in enumerate(((c_hi, c_lo), (y_hi, y_lo))):
                    if k == 1:
                        eng.wait_ge(s_yd[g], 64 * (c + 1))
                    for w, src in ((cw_hi, hi), (cw_hi, lo), (cw_lo, hi)):
                        last = mm(p_conv[:, :], w[:, k, g, :], runs(src, g), start=(n == 0), stop=(n == 5))
                        n += 1
                last.then_inc(s_conv, 1)

            def transpose_u(c, g):
                eng.wait_ge(s_u, G * c + g + 1)
                if c or g:
                    eng.wait_ge(s_utl, G * c + g)
                for n in range(UB):
                    last = eng.transpose(p_ut[:, n * P:(n + 1) * P], u_sb[:, g % 2, n * P:(n + 1) * P], ident[:, :])
                last.then_inc(s_ut, 1)

            def linear(d, slot):
                f, q = slot // 4, slot % 4
                t, j = f // 2, f % 2
                if q == 0:
                    if f == 0:
                        if d == 0:
                            eng.wait_ge(s_wf, 2)
                        eng.wait_ge(s_utl, G * (d + 1))
                    if d or f >= 2:
                        eng.wait_ge(s_res, 4 * d + f - 1)
                if q == 3:
                    with eng.If(inexact != 0):
                        for r in range(R):
                            for u in (u_hi, u_lo):
                                for w in (rest_hi, rest_lo):
                                    mm(p_f[f % 2][:, :], u[:, d % 2, r, t * P:(t + 1) * P],
                                       w[:, :].unsqueeze(1).broadcast_to([P, HALF // P, P]), start=False, stop=False)
                for r in (2 * q, 2 * q + 1):
                    for u in (u_hi, u_lo):
                        last = mm(p_f[f % 2][:, :], u[:, d % 2, r, t * P:(t + 1) * P], w_ffn[:, r, j * HALF:(j + 1) * HALF],
                                  start=(r == 0 and u is u_hi), stop=(r == R - 1 and u is u_lo))
                if q == 3:
                    last.then_inc(s_f, 1)

            for i in range(NI):
                a, b, c, d = i, i - 1, i - 2, i - 3
                for slot in range(SLOTS):
                    if 0 <= d < NU:
                        linear(d, slot)
                    if a < NU and slot < 4:
                        transpose_x(a, slot)
                    if 0 <= c < NU and slot % 4 == 0:
                        conv(c, slot // 4)
                    if 0 <= c < NU and slot % 4 == 2:
                        transpose_u(c, slot // 4)
                    if 0 <= b < NU and slot == 3:
                        transpose_o(b)
                    if a < NU and slot in (3, 5):
                        project(a, (slot - 3) // 2)
                    if a < NU and slot in (6, 7):
                        mix(a, slot - 6)
                    if 0 <= b < NU and slot in (7, 9, 11, 13):
                        transpose_x1(b, (slot - 7) // 2)


def kernel(**inputs):
    import numpy as np
    from concourse import bacc
    from concourse.bass_utils import run_bass_kernel_spmd

    def arr(name):
        return np.asarray(inputs[name])

    conv_w = arr("L0_cond2_weight").reshape(G, CG, CG, TAPS).transpose(2, 0, 3, 1)[:, :, ::-1, :]
    ctx_w = arr("L0_cond2_c_weight").T.reshape(P, G, 1, CG)
    arrays = {
        "x": arr("x").reshape(B * S, D),
        "cond_t": arr("cond_128").T,
        "w0": arr("L0_cond_W0"), "b0": arr("L0_cond_b0").reshape(P, 1),
        "w1": arr("L0_cond_W1"), "b1": arr("L0_cond_b1").reshape(P, 1),
        "w2": arr("L0_cond_W2"), "b2": arr("L0_cond_b2").reshape(1, KE),
        "mix_w": arr("L0_cond_weight").reshape(KE, S, S).transpose(0, 2, 1).reshape(KE, S * S),
        "mix_b": arr("L0_cond_bias_k"),
        "wq": arr("L0_attn_Wq").reshape(P, R, DH * NH), "bq": arr("L0_attn_bq").reshape(1, DH * NH),
        "wk": arr("L0_attn_Wk").reshape(P, R, DH), "bk": arr("L0_attn_bk").reshape(1, DH),
        "wv": arr("L0_attn_Wv").reshape(P, R, DH), "bv": arr("L0_attn_bv").reshape(1, DH),
        "conv_w": conv_w.reshape(CG, G, TAPS * CG),
        "ctx_w": np.broadcast_to(ctx_w, (P, G, R, CG)).reshape(P, G, P),
        "conv_bias": np.tile(arr("fside_S_0").reshape(G, CG).T, (R, 1)),
        "packed_t": arr("L0_ffn_packed_weight").T.reshape(P, R, HALF),
        "scale": arr("L0_ffn_scale").reshape(1, 1), "zero_point": arr("L0_ffn_zero_point").reshape(1, 1),
        "ffn_bias": arr("L0_ffn_bias").reshape(1, D),
    }
    nc = bacc.Bacc("TRN2", target_bir_lowering=False, num_devices=1)
    args = {}
    for name, a in arrays.items():
        arrays[name] = a = np.ascontiguousarray(a)
        args[name] = nc.dram_tensor(name + "_in", a.shape, mybir.dt.from_np(a.dtype), kind="ExternalInput").ap()
    args["out"] = nc.dram_tensor("out_0", (B * S, D), F32, kind="ExternalOutput").ap()
    block_program(nc, **args)
    r = run_bass_kernel_spmd(nc, [{name + "_in": a for name, a in arrays.items()}], core_ids=[0])
    return r.results[0]["out_0"].reshape(B, S, D)
```

```python
import concourse.bass as bass
from concourse import mybir
from contextlib import ExitStack

F32 = mybir.dt.float32
F32R = mybir.dt.float32r
I32 = mybir.dt.int32
U8 = mybir.dt.uint8
ALU = mybir.AluOpType
ACT = mybir.ActivationFunctionType
AX = mybir.AxisListType

P = 128
B, S, D = 64, 64, 1024
DH, NH = 32, 32
KE = 8
R = D // P
G, CG = 4, 16
TAPS, PAD = 9, 4
UB = 4
TU = 2
UT = UB * S
NU = B // UB
NT = NU * TU
SLOTS = 16
W3 = 3 * DH
COLS = 1 + G * UB * (P + 1)
HALF = D // 2
ZLIM = 1000.0
NX = 5


COLS_AT = {"cond": (0, B), "w0": (B, P), "w1": (B + P, P), "w2": (B + 2 * P, KE), "b0": (B + 2 * P + KE, 1),
           "b1": (B + 2 * P + KE + 1, 1), "cbias": (B + 2 * P + KE + 2, G)}
NCOLS = B + 2 * P + KE + 2 + G
ROW_AT = {"scale": 0, "zero": 1, "b2": 2, "bk": 2 + KE, "bv": 2 + KE + DH}
NROW = 2 + KE + 2 * DH


def block_program(nc, x, cols, row, mix_w, wq, bq, wkv, conv_w, ctx_w, packed_t, ffn_bias, out):
    ctx = ExitStack()
    with ctx:
        def sb(name, shape, dt=F32):
            return ctx.enter_context(nc.sbuf_tensor(name, shape, dt))

        def ps(name):
            return ctx.enter_context(nc.psum_tensor(name, [P, 512], F32))

        def sem(name):
            return ctx.enter_context(nc.semaphore(name))

        x_nat = sb("x_nat", [P, NX, TU, D])
        x_t = sb("x_t", [P, 2, R, UT])
        x1_t = sb("x1_t", [P, UT // CG, R, CG])
        w3 = sb("w3", [P, R, W3])
        z_sb = sb("z_sb", [P, TU, W3])
        qkv_bias = sb("qkv_bias", [P, TU, W3])
        qkv = sb("qkv", [P, TU, W3])
        prob = sb("prob", [P, TU, DH, DH])
        k_max = sb("k_max", [P, TU])
        k_min = sb("k_min", [P, TU])
        top = sb("top", [P, TU, DH])
        top2 = sb("top2", [P, TU, DH])
        den = sb("den", [P, TU, DH])
        rden = sb("rden", [P, TU, DH])
        num = sb("num", [P, TU, DH])
        o_rep = sb("o_rep", [P, TU, DH, 4])
        o_t = sb("o_t", [P, UT])
        c_in = sb("c_in", [P, 2, COLS], F32R)
        y_in = sb("y_in", [P, 2, COLS], F32R)
        c_hi, c_lo, y_hi, y_lo = c_in[:, 0, :], c_in[:, 1, :], y_in[:, 0, :], y_in[:, 1, :]
        u_sb = sb("u_sb", [P, 2, UB * P])
        u_hi = sb("u_hi", [P, 2, R, UT], F32R)
        u_lo = sb("u_lo", [P, 2, R, UT], F32R)
        w_ffn = sb("w_ffn", [P, R, D], F32R)
        cw_hi = sb("cw_hi", [P, 2, G, P], F32R)
        cw_lo = sb("cw_lo", [P, 2, G, P], F32R)
        mix_t = sb("mix_t", [P, NT, S])
        ffn_b = sb("ffn_b", [P, D])
        rest_hi = sb("rest_hi", [P, P], F32R)
        rest_lo = sb("rest_lo", [P, P], F32R)
        ident = sb("ident", [P, P])
        ones = sb("ones", [P, P])
        cols_sb = sb("cols_sb", [P, NCOLS])
        row_sb = sb("row_sb", [P, NROW])
        cond_sb, w0_sb, w1_sb, w2_sb, b0_sb, b1_sb, cbias_sb = (
            cols_sb[:, at:at + n] for at, n in COLS_AT.values())
        sc = row_sb[:, 0:1]
        b2_sb = row_sb[0:B, ROW_AT["b2"]:ROW_AT["b2"] + KE]
        h_sb = sb("h_sb", [P, 2, B])
        att = sb("att", [B, 4, KE])
        att_s = sb("att_s", [B, 4])
        att_t = sb("att_t", [KE, B])
        mix_bias = sb("mix_bias", [P, NT])
        u_bias = sb("u_bias", [P, G, B])
        zp = sb("zp", [P, 5])
        zi = sb("zi", [P, 1], I32)
        flag = sb("flag", [1, 2], I32)
        bias3 = sb("bias3", [P, W3])
        col3 = sb("col3", [P, W3])
        cw = u_sb[:, :, :].rearrange("p y (g n) -> p y g n", g=G)
        spare = x1_t[:, :, :, :].rearrange("p b r c -> p (b r c)")
        mixw_lo = spare[0:KE, :]
        mixw_hi = x_t[0:KE, 1, :, :].rearrange("k r t -> k (r t)")
        mixed_lo = prob[0:B, :, :, :].rearrange("b t d e -> b (t d e)")
        mixed_hi = spare[0:B, :]
        packed = spare[:, 0:1024].bitcast(U8).rearrange("p (r n) -> p r n", n=HALF)
        low4 = spare[:, 1024:2048].bitcast(U8).rearrange("p (r n) -> p r n", n=HALF)
        ctx_sb = (o_rep[:, :, :, :].rearrange("p t d e -> p t (d e)"),
                  o_t[:, :].rearrange("p (t n) -> p t n", t=2))
        mixb_sb = qkv[0:KE, :, :].rearrange("k t w -> k (t w)")[:, 0:P]
        bq_tmp = ffn_b[:, :].rearrange("p (d h) -> p d h", h=NH)

        p_xt, p_z, p_sm, p_x2, p_conv, p_ut = (ps(n) for n in ("p_xt", "p_z", "p_sm", "p_x2", "p_conv", "p_ut"))
        p_f = [ps("p_f0"), ps("p_f1")]

        mixed_dram = nc.dram_tensor("mixed_dram", [B, S * S], F32).ap()

        s_small = sem("s_small")
        s_small2 = sem("s_small2")
        s_wq = [sem(f"s_wq{i}") for i in range(4)]
        s_wkv = sem("s_wkv")
        s_mw = sem("s_mw")
        s_pk = sem("s_pk")
        s_cw = sem("s_cw")
        s_x = [sem(f"s_xload{i}") for i in range(NX)]
        s_out = [sem(f"s_out{i}") for i in range(NX)]
        s_yd = [sem(f"s_yd{g}") for g in range(G)]
        s_pool0 = sem("s_pool0")
        s_pe0 = sem("s_pe0")
        s_act0 = sem("s_act0")
        s_dve0 = sem("s_dve0")
        s_mixed = sem("s_mixed")
        s_mixedc = sem("s_mixedc")
        s_mixedd = sem("s_mixedd")
        s_mixt = sem("s_mixt")
        s_bq = sem("s_bq")
        s_bqr = sem("s_bqr")
        s_ffb = sem("s_ffb")
        s_w3 = sem("s_w3")
        s_wf = sem("s_wf")
        s_xt = sem("s_xt")
        s_xtc = sem("s_xtc")
        s_z = sem("s_z")
        s_zc = sem("s_zc")
        s_mix = sem("s_mix")
        s_qb = sem("s_qb")
        s_qkv = sem("s_qkv")
        s_top = sem("s_top")
        s_score = sem("s_score")
        s_sub = sem("s_sub")
        s_exp = sem("s_exp")
        s_den = sem("s_den")
        s_pv = sem("s_pv")
        s_num = sem("s_num")
        s_o = sem("s_o")
        s_ot = sem("s_ot")
        s_otc = sem("s_otc")
        s_x1t = sem("s_x1t")
        s_xb = sem("s_xb")
        s_x1 = sem("s_x1")
        s_x2 = sem("s_x2")
        s_x2h = sem("s_x2h")
        s_x2l = sem("s_x2l")
        s_conv = sem("s_conv")
        s_u = sem("s_u")
        s_ut = sem("s_ut")
        s_uth = sem("s_uth")
        s_utl = sem("s_utl")
        s_f = sem("s_f")
        s_res = sem("s_res")

        block = ctx.enter_context(nc.Block())

        def xbuf(u):
            return x_nat[:, u % NX, :, :]

        def col(g, n):
            return 1 + (g * UB + n) * (P + 1)

        def runs(t, g):
            return t[:, col(g, 0):col(g, 0) + UB * (P + 1)].rearrange("p (n c) -> p n c", c=P + 1)[:, :, 0:P]

        def ut_view(t, u, g):
            v = t[:, u % 2, :, :].rearrange("p r (n c) -> p n r c", n=UB)
            return v[:, :, :, g * CG:(g + 1) * CG]

        N_SMALL, N_SMALL2 = 3, 2
        N_CW = 2 * R
        NI = NU + 4

        XT_SLOT, Z_SLOT, MIX_SLOT = (0, 1, 2, 3), (4, 6), (7, 8)
        TOP_SLOT, SCORE_SLOT, SUB_SLOT, EXP_SLOT = 8, (9, 11), (10, 12), (11, 13)
        DEN_SLOT, PV_SLOT, BIAS_SLOT = (12, 14), (13, 15), 11
        X2_SLOT, X1_SLOT = (8, 10, 12, 14), 8
        CONV_SLOT, UT_SLOT = (0, 3, 6, 9), (2, 5, 8, 11)
        FINISH_SLOT = (4, 8, 12)

        def O_SLOT(i):
            return 4 if i > 1 else 6

        @block.sync
        def _(eng):
            def load_x(u):
                if u >= NX:
                    eng.wait_ge(s_out[u % NX], 32 * (u // NX))
                for t in range(TU):
                    row = (u * TU + t) * P
                    eng.dma_start(x_nat[:, u % NX, t, :], x[row:row + P, :]).then_inc(s_x[u % NX], 16)

            def store(d, t):
                eng.wait_ge(s_res, 4 * d + 2 * t + 2)
                row = (d * TU + t) * P
                eng.dma_start(out[row:row + P, :], x_nat[:, d % NX, t, :]).then_inc(s_out[d % NX], 16)

            for c in range(4):
                if c == 2:
                    load_x(0)
                eng.dma_start(x_nat[:, 1 + c, :, :], wq[:, 2 * c:2 * c + 2, :]).then_inc(s_wq[c], 16)
            eng.dma_start(w3[:, :, DH:W3], wkv).then_inc(s_wkv, 16)
            for j, src in enumerate((mixed_lo, mixed_hi)):
                eng.wait_ge(s_mixedc, 4 * (j + 1))
                eng.dma_start(mixed_dram[:, 2048 * j:2048 * j + 2048], src).then_inc(s_mixedd, 16)
            eng.wait_ge(s_mixedd, 32)
            for h in range(2):
                eng.dma_start(mix_t[h * S:h * S + S, :, :],
                              mixed_dram.rearrange("(t h) (i s) -> h i t s", h=2, i=S)[h]).then_inc(s_mixt, 16)
            eng.dma_start(packed, packed_t).then_inc(s_pk, 16)
            eng.wait_ge(s_bqr, 1)
            eng.dma_start(ffn_b[:, :], ffn_bias.broadcast_to([P, D])).then_inc(s_ffb, 16)

            for i in range(NI):
                a, b, d = i, i - 1, i - 3
                for slot in range(SLOTS):
                    if slot == 2 and 0 <= d - 1 < NU:
                        store(d - 1, 1)
                    if slot == 3 and a + 1 < NU:
                        if 1 <= a + 1 < NX:
                            eng.wait_ge(s_w3, a + 1)
                        load_x(a + 1)
                    if 0 <= b < NU and slot in X2_SLOT:
                        g = X2_SLOT.index(slot)
                        eng.wait_ge(s_x2h, G * b + g + 1)
                        eng.wait_ge(s_x2l, G * b + g + 1)
                        if b:
                            eng.wait_ge(s_conv, G * (b - 1) + g + 1)
                        c0, n = col(g, 0), UB * (P + 1) - 1
                        src, dst = c_in[:, :, :].bitcast(F32), y_in[:, :, :].bitcast(F32)
                        eng.dma_start(dst[0:64, :, c0:c0 + n], src[0:64, :, c0 + 1:c0 + 1 + n]).then_inc(s_yd[g], 16)
                        eng.dma_start(dst[64:P, :, c0:c0 + n], src[64:P, :, c0 - 1:c0 - 1 + n]).then_inc(s_yd[g], 16)
                    if 0 <= d < NU and slot == 9:
                        store(d, 0)
            for k in range(NX):
                eng.wait_ge(s_out[k], 32 * len(range(k, NU, NX)))

        @block.gpsimd
        def _(eng):
            eng.memset(ident[:, :], 0.0).then_inc(s_pool0, 1)
            eng.memset(u_sb[:, :, :], 0.0).then_inc(s_pool0, 1)
            eng.memset(ones[:, :], 1.0).then_inc(s_pool0, 1)
            eng.wait_ge(s_pool0, 3)
            eng.affine_select(out=ident[:, :], in_=ident[:, :], compare_op=ALU.not_equal, fill=1.0,
                              base=0, pattern=[[-1, P]], channel_multiplier=1).then_inc(s_pool0, 1)
            for t in (c_in, y_in):
                eng.memset(t[:, :, 0:COLS:P + 1].bitcast(F32), 0.0).then_inc(s_pool0, 1)
            for r in range(R):
                lo, hi = max(0, r - PAD), min(R - 1, r + PAD)
                eng.dma_start(cw[r * CG:(r + 1) * CG, 0, :, lo * CG:(hi + 1) * CG],
                              conv_w[:, :, (lo - r + PAD) * CG:(hi - r + PAD + 1) * CG]).then_inc(s_cw, 16)
                lo, hi, k = (r + PAD, R - 1, 0) if r < PAD else (0, r - PAD, 12 - r)
                eng.dma_start(cw[r * CG:(r + 1) * CG, 1, :, lo * CG:(hi + 1) * CG],
                              conv_w[:, :, k * CG:(k + hi - lo + 1) * CG]).then_inc(s_cw, 16)

            for i in range(NI):
                a, b = i, i - 1
                for slot in range(SLOTS):
                    if 0 <= b < NU and slot == O_SLOT(i) + 1:
                        eng.wait_ge(s_otc, b + 1)
                        if b:
                            eng.wait_ge(s_x2, G * b)
                        else:
                            eng.wait_ge(s_wf, 2)
                        eng.tensor_tensor(x1_t[:, :, :, :].rearrange("p b r c -> p r b c"),
                                          x_t[:, b % 2, :, :].rearrange("p r (b c) -> p r b c", c=CG),
                                          o_t[:, :].rearrange("p (b c) -> p b c", c=CG).unsqueeze(1).broadcast_to([P, R, UT // CG, CG]),
                                          ALU.add).then_inc(s_x1t, 1)
                    if 0 <= b < NU and slot == X1_SLOT:
                        eng.wait_ge(s_xb, b + 1)
                        eng.wait_ge(s_o, b + 1)
                        xv = xbuf(b).rearrange("p t (d h) -> p t d h", h=NH)
                        eng.tensor_tensor(xv, xv, o_rep[:, :, :, 0:1].broadcast_to([P, TU, DH, NH]), ALU.add).then_inc(s_x1, 1)
                    if a < NU and slot == BIAS_SLOT:
                        if a == 0:
                            eng.wait_ge(s_ffb, 16)
                        eng.wait_ge(s_xt, 4 * (a + 1))
                        eng.tensor_tensor(xbuf(a), xbuf(a), ffn_b[:, :].unsqueeze(1).broadcast_to([P, TU, D]), ALU.add).then_inc(s_xb, 1)

        @block.scalar
        def _(eng):
            eng.dma_start(cols_sb[:, :], cols).then_inc(s_small, 16)
            eng.dma_start(row_sb[:, :], row.broadcast_to([P, NROW])).then_inc(s_small, 16)
            eng.dma_start(mixb_sb, mix_w[:, 0:P]).then_inc(s_small, 16)
            eng.dma_start(mixw_lo, mix_w[:, P:P + 2048]).then_inc(s_mw, 16)
            eng.dma_start(mixw_hi, mix_w[:, P + 2048:P + 4096]).then_inc(s_mw, 16)
            eng.dma_start(bq_tmp, bq.broadcast_to([P, DH * NH]).rearrange("p (d h) -> p d h", h=NH)).then_inc(s_bq, 16)
            for n in range(2):
                eng.dma_start(ctx_sb[n], ctx_w[:, 2 * n:2 * n + 2, :]).then_inc(s_small2, 16)
            for n, bias in enumerate((b0_sb, b1_sb)):
                eng.wait_ge(s_pe0, n + 1)
                eng.activation(h_sb[:, n, :], p_sm[:, 64 * n:64 * n + 64], ACT.Gelu, bias=bias).then_inc(s_act0, 1)
            eng.wait_ge(s_dve0, 3)
            eng.activation(att[:, 1, :], att[:, 0, :], ACT.Exp, accum_out=att_s[:, 2:3]).then_inc(s_act0, 1)
            for c in range(8):
                eng.wait_ge(s_mixed, c + 1)
                dst = (mixed_lo, mixed_hi)[c // 4]
                eng.activation(dst[:, 512 * (c % 4):512 * (c % 4) + 512], p_f[c % 2][0:B, :], ACT.Copy).then_inc(s_mixedc, 1)

            def xt_copy(a, k):
                eng.wait_ge(s_xt, 4 * a + k + 1)
                if a >= 2 and k == 0:
                    eng.wait_ge(s_x1t, a - 1)
                t, r0 = k // 2, 4 * (k % 2)
                eng.activation(x_t[:, a % 2, r0:r0 + 4, t * P:(t + 1) * P],
                               p_xt[:, :].rearrange("p (r t) -> p r t", t=P), ACT.Copy).then_inc(s_xtc, 1)

            def z_copy(a, t):
                eng.wait_ge(s_z, TU * a + t + 1)
                if a:
                    eng.wait_ge(s_mix, TU * (a - 1) + t + 1)
                eng.activation(z_sb[:, t, :], p_z[:, 0:W3], ACT.Copy).then_inc(s_zc, 1)

            def o_copy(b):
                eng.wait_ge(s_ot, b + 1)
                if b:
                    eng.wait_ge(s_x1t, b)
                eng.activation(o_t[:, :], p_sm[:, 192:192 + UT], ACT.Copy).then_inc(s_otc, 1)

            def x2_hi(b, g):
                eng.wait_ge(s_x2, G * b + g + 1)
                if b:
                    eng.wait_ge(s_conv, G * (b - 1) + g + 1)
                eng.activation(runs(c_hi, g), p_x2[:, :].rearrange("p (n c) -> p n c", n=UB), ACT.Copy).then_inc(s_x2h, 1)

            def ut_hi(c, g):
                eng.wait_ge(s_ut, G * c + g + 1)
                if c >= 2:
                    eng.wait_ge(s_f, 4 * (c - 1))
                eng.activation(ut_view(u_hi, c, g),
                               p_ut[:, :].rearrange("p (n r c) -> p n r c", n=UB, r=R), ACT.Copy).then_inc(s_uth, 1)

            def u_copy(c, g):
                eng.wait_ge(s_conv, G * c + g + 1)
                if c or g >= 2:
                    eng.wait_ge(s_ut, G * c + g - 1)
                elif g == 0:
                    eng.wait_ge(s_dve0, 17)
                for n in range(UB):
                    ins = eng.activation(u_sb[:, g % 2, n * P:(n + 1) * P], p_conv[:, n * P:(n + 1) * P], ACT.Identity,
                                         bias=u_bias[:, g, UB * c + n:UB * c + n + 1], scale=sc)
                ins.then_inc(s_u, 1)

            for i in range(NI):
                a, b, c = i, i - 1, i - 2
                for slot in range(SLOTS):
                    if a < NU and slot in XT_SLOT:
                        xt_copy(a, XT_SLOT.index(slot))
                    if 0 <= c < NU and slot in UT_SLOT:
                        ut_hi(c, UT_SLOT.index(slot))
                    if 0 <= b < NU and slot in X2_SLOT:
                        x2_hi(b, X2_SLOT.index(slot))
                    if 0 <= b < NU and slot == O_SLOT(i):
                        o_copy(b)
                    if a < NU and slot in Z_SLOT:
                        z_copy(a, Z_SLOT.index(slot))
                    if 0 <= c < NU and slot in CONV_SLOT:
                        u_copy(c, CONV_SLOT.index(slot))
                    if a < NU and slot in EXP_SLOT:
                        t = EXP_SLOT.index(slot)
                        eng.wait_ge(s_sub, TU * a + t + 1)
                        flat = prob[:, t, :, :].rearrange("p d e -> p (d e)")
                        eng.activation(flat, flat, ACT.Exp, scale=float(DH) ** -0.5).then_inc(s_exp, 1)
                if i == 0:
                    for half, src in enumerate((low4, packed)):
                        eng.wait_ge(s_dve0, 19 + half)
                        eng.activation(w_ffn[:, :, half:D:2], src, ACT.Identity, bias=zp[:, 4:5]).then_inc(s_wf, 1)

        @block.vector
        def _(eng):
            def chunk_sum(c):
                eng.wait_ge(s_wq[c], 16)
                eng.tensor_reduce(w3[:, 2 * c:2 * c + 2, 0:DH],
                                  x_nat[:, 1 + c, :, :].rearrange("p t (d h) -> p t d h", h=NH), AX.X, ALU.add).then_inc(s_w3, 1)

            eng.wait_ge(s_small, 16 * N_SMALL)
            eng.wait_ge(s_pe0, 3)
            eng.tensor_tensor(att[:, 0, :], p_sm[0:B, 128:128 + KE], b2_sb, ALU.add).then_inc(s_dve0, 1)
            eng.wait_ge(s_dve0, 1)
            eng.tensor_reduce(att_s[:, 0:1], att[:, 0, :], AX.X, ALU.max).then_inc(s_dve0, 1)
            eng.wait_ge(s_dve0, 2)
            eng.tensor_scalar(att[:, 0, :], att[:, 0, :], att_s[:, 0:1], None, ALU.subtract).then_inc(s_dve0, 1)
            eng.wait_ge(s_act0, 3)
            eng.reciprocal(att_s[:, 3:4], att_s[:, 2:3]).then_inc(s_dve0, 1)
            eng.wait_ge(s_dve0, 4)
            eng.tensor_scalar(att[:, 2, :], att[:, 1, :], att_s[:, 3:4], None, ALU.mult).then_inc(s_dve0, 1)
            eng.wait_ge(s_pe0, 4)
            eng.tensor_copy(att_t[:, :], p_sm[0:KE, 192:192 + B]).then_inc(s_dve0, 1)
            eng.wait_ge(s_pe0, 5)
            for h in range(2):
                eng.tensor_copy(mix_bias[h * S:h * S + S, :], p_sm[h * S:h * S + S, 256 + h:256 + B:2]).then_inc(s_dve0, 1)
            zero = row_sb[:, ROW_AT["zero"]:ROW_AT["zero"] + 1]
            eng.tensor_scalar(zp[:, 1:2], zero, ZLIM, -ZLIM, ALU.min, ALU.max).then_inc(s_dve0, 1)
            eng.wait_ge(s_dve0, 9)
            eng.tensor_copy(zi[:, :], zp[:, 1:2]).then_inc(s_dve0, 1)
            eng.wait_ge(s_dve0, 10)
            eng.tensor_copy(zp[:, 2:3], zi[:, :]).then_inc(s_dve0, 1)
            eng.wait_ge(s_dve0, 11)
            eng.tensor_tensor(zp[:, 3:4], zp[:, 2:3], zero, ALU.subtract).then_inc(s_dve0, 1)
            eng.tensor_scalar(zp[:, 4:5], zp[:, 2:3], -1.0, None, ALU.mult).then_inc(s_dve0, 1)
            eng.wait_ge(s_dve0, 13)
            rest = zp[:, 3:4].broadcast_to([P, P])
            eng.tensor_scalar(flag[0:1, 0:1], zp[0:1, 3:4], 0.0, None, ALU.not_equal).then_inc(s_dve0, 1)
            eng.tensor_copy(rest_hi[:, :], rest).then_inc(s_dve0, 1)
            eng.wait_ge(s_dve0, 15)
            eng.tensor_tensor(rest_lo[:, :], rest, rest_hi[:, :].bitcast(F32), ALU.subtract).then_inc(s_dve0, 1)
            eng.wait_ge(s_pe0, 6)
            for g in range(G):
                ins = eng.tensor_scalar(u_bias[:, g, :], p_conv[:, B * g:B * g + B], cbias_sb[:, g:g + 1], sc, ALU.add, ALU.mult)
            ins.then_inc(s_dve0, 1)
            eng.wait_ge(s_bq, 16)
            eng.tensor_reduce(bias3[:, 0:DH], bq_tmp, AX.X, ALU.add).then_inc(s_bqr, 1)
            eng.tensor_copy(bias3[:, DH:W3], row_sb[:, ROW_AT["bk"]:ROW_AT["bk"] + 2 * DH]).then_inc(s_bqr, 1)
            for c in range(4):
                chunk_sum(c)
            eng.wait_ge(s_pe0, 7)
            eng.tensor_copy(col3[:, :], p_sm[:, 320:320 + W3]).then_inc(s_dve0, 1)
            eng.wait_ge(s_pk, 16)
            eng.tensor_scalar(low4, packed, 15, None, ALU.bitwise_and).then_inc(s_dve0, 1)
            eng.wait_ge(s_dve0, 19)
            eng.tensor_scalar(packed, packed, 4, None, ALU.logical_shift_right).then_inc(s_dve0, 1)
            eng.wait_ge(s_cw, 16 * N_CW)
            eng.tensor_copy(cw_hi[:, :, :, :], cw).then_inc(s_dve0, 1)
            eng.wait_ge(s_dve0, 21)
            eng.tensor_tensor(cw_lo[:, :, :, :], cw, cw_hi[:, :, :, :].bitcast(F32), ALU.subtract).then_inc(s_dve0, 1)

            def softmax_top(a):
                q, k = qkv[:, :, 0:DH], qkv[:, :, DH:2 * DH]
                eng.wait_ge(s_qkv, a + 1)
                for dst, op in ((k_max, ALU.max), (k_min, ALU.min)):
                    eng.tensor_reduce(dst[:, :], k, AX.X, op).then_inc(s_top, 1)
                for n, (dst, src) in enumerate(((top, k_max), (top2, k_min))):
                    eng.wait_ge(s_top, 5 * a + n + 1)
                    eng.tensor_tensor(dst[:, :, :], q, src[:, :].unsqueeze(2).broadcast_to([P, TU, DH]), ALU.mult).then_inc(s_top, 1)
                eng.wait_ge(s_top, 5 * a + 4)
                eng.tensor_tensor(top[:, :, :], top[:, :, :], top2[:, :, :], ALU.max).then_inc(s_top, 1)

            def down(v):
                return v.unsqueeze(2).broadcast_to([P, DH, DH])

            def along(v):
                return v.unsqueeze(1).broadcast_to([P, DH, DH])

            def score(a, t):
                eng.tensor_tensor(prob[:, t, :, :], down(qkv[:, t, 0:DH]), along(qkv[:, t, DH:2 * DH]), ALU.mult).then_inc(s_score, 1)

            def subtract(a, t):
                eng.wait_ge(s_score, TU * a + t + 1)
                eng.wait_ge(s_top, 5 * a + 5)
                eng.tensor_tensor(prob[:, t, :, :], prob[:, t, :, :], down(top[:, t, :]), ALU.subtract).then_inc(s_sub, 1)

            def sum_exp(a, t):
                eng.wait_ge(s_exp, TU * a + t + 1)
                eng.tensor_reduce(den[:, t, :], prob[:, t, :, :], AX.X, ALU.add).then_inc(s_den, 1)

            def times_v(a, t):
                eng.wait_ge(s_den, TU * a + t + 1)
                eng.tensor_tensor(prob[:, t, :, :], prob[:, t, :, :], along(qkv[:, t, 2 * DH:]), ALU.mult).then_inc(s_pv, 1)

            def sum_v(b, t):
                eng.wait_ge(s_pv, TU * b + t + 1)
                eng.tensor_reduce(num[:, t, :], prob[:, t, :, :], AX.X, ALU.add).then_inc(s_num, 1)

            def divide(b):
                eng.wait_ge(s_den, TU * b + 2)
                eng.reciprocal(rden[:, :, :], den[:, :, :]).then_inc(s_num, 1)
                eng.wait_ge(s_num, 3 * b + 3)
                if b:
                    eng.wait_ge(s_ot, b)
                    eng.wait_ge(s_x1, b)
                eng.tensor_tensor(o_rep[:, :, :, :], num[:, :, :].unsqueeze(3).broadcast_to([P, TU, DH, 4]),
                                  rden[:, :, :].unsqueeze(3).broadcast_to([P, TU, DH, 4]), ALU.mult).then_inc(s_o, 1)

            def finish(d, f):
                t, j = f // 2, f % 2
                eng.wait_ge(s_f, 4 * d + f + 1)
                if f == 0:
                    eng.wait_ge(s_x1, d + 1)
                part = x_nat[:, d % NX, t, j * HALF:(j + 1) * HALF]
                eng.tensor_tensor(part, p_f[f % 2][:, :], part, ALU.add).then_inc(s_res, 1)

            for i in range(NI):
                a, b, c, d = i, i - 1, i - 2, i - 3
                for slot in range(SLOTS):
                    if slot == 0 and 0 <= d - 1 < NU:
                        finish(d - 1, 3)
                    if slot in FINISH_SLOT and 0 <= d < NU:
                        finish(d, FINISH_SLOT.index(slot))
                    if 0 <= c < NU and slot in UT_SLOT:
                        g = UT_SLOT.index(slot)
                        eng.wait_ge(s_uth, G * c + g + 1)
                        eng.tensor_tensor(ut_view(u_lo, c, g), p_ut[:, :].rearrange("p (n r c) -> p n r c", n=UB, r=R),
                                          ut_view(u_hi, c, g).bitcast(F32), ALU.subtract).then_inc(s_utl, 1)
                    if 0 <= b < NU and slot in X2_SLOT:
                        g = X2_SLOT.index(slot)
                        eng.wait_ge(s_x2h, G * b + g + 1)
                        eng.tensor_tensor(runs(c_lo, g), p_x2[:, :].rearrange("p (n c) -> p n c", n=UB),
                                          runs(c_hi, g).bitcast(F32), ALU.subtract).then_inc(s_x2l, 1)
                    if a < NU and slot == TOP_SLOT:
                        for t in range(TU):
                            eng.scalar_tensor_tensor(out=qkv_bias[:, t, :], in0=col3[:, :], scalar=mix_bias[:, TU * a + t:TU * a + t + 1],
                                                     in1=bias3[:, :], op0=ALU.mult, op1=ALU.add).then_inc(s_qb, 1)
                        eng.wait_ge(s_qb, TU * (a + 1))
                        eng.wait_ge(s_mix, TU * (a + 1))
                        eng.tensor_tensor(qkv[:, :, :], p_sm[:, 0:TU * W3].rearrange("p (t w) -> p t w", t=TU),
                                          qkv_bias[:, :, :], ALU.add).then_inc(s_qkv, 1)
                        softmax_top(a)
                    if a < NU:
                        for at, what in ((SCORE_SLOT, score), (SUB_SLOT, subtract), (DEN_SLOT, sum_exp), (PV_SLOT, times_v)):
                            if slot in at:
                                what(a, at.index(slot))
                        if slot == SLOTS - 1:
                            sum_v(a, 0)
                    if 0 <= b < NU and slot == 0:
                        sum_v(b, 1)
                    if 0 <= b < NU and slot == 1:
                        divide(b)

        @block.tensor
        def _(eng):
            mm = eng.matmul
            eng.wait_ge(s_small, 16 * N_SMALL)
            mm(p_sm[:, 0:B], w0_sb, cond_sb, start=True, stop=True).then_inc(s_pe0, 1)
            eng.wait_ge(s_act0, 1)
            mm(p_sm[:, B:2 * B], w1_sb, h_sb[:, 0, :], start=True, stop=True).then_inc(s_pe0, 1)
            eng.wait_ge(s_act0, 2)
            mm(p_sm[0:B, 128:128 + KE], h_sb[:, 1, :], w2_sb, start=True, stop=True).then_inc(s_pe0, 1)
            eng.wait_ge(s_dve0, 5)
            eng.wait_ge(s_pool0, 4)
            eng.transpose(p_sm[0:KE, 192:192 + B], att[:, 2, :], ident[0:B, 0:B]).then_inc(s_pe0, 1)
            eng.wait_ge(s_dve0, 6)
            mm(p_sm[:, 256:256 + B], mixb_sb, att_t[:, :], start=True, stop=True).then_inc(s_pe0, 1)
            eng.wait_ge(s_mw, 32)
            for c in range(8):
                if c >= 2:
                    eng.wait_ge(s_mixedc, c - 1)
                src = (mixw_lo, mixw_hi)[c // 4]
                mm(p_f[c % 2][0:B, :], att_t[:, :], src[:, 512 * (c % 4):512 * (c % 4) + 512],
                   start=True, stop=True).then_inc(s_mixed, 1)
            eng.wait_ge(s_small2, 16 * N_SMALL2)
            for g in range(G):
                last = mm(p_conv[:, B * g:B * g + B], ctx_sb[g // 2][:, g % 2, :], cond_sb, start=True, stop=True)
            last.then_inc(s_pe0, 1)
            eng.wait_ge(s_dve0, 14)
            inexact = eng.value_load(flag[0:1, 0:1], min_val=0, max_val=1)

            def transpose_x(a, k):
                if k == 0:
                    eng.wait_ge(s_x[a % NX], 32 * (a // NX + 1))
                if a or k:
                    eng.wait_ge(s_xtc, 4 * a + k)
                t, r0 = k // 2, 4 * (k % 2)
                for r in range(4):
                    last = eng.transpose(p_xt[:, r * P:(r + 1) * P], x_nat[:, a % NX, t, r0 + r:D:R], ident[:, :])
                last.then_inc(s_xt, 1)

            def project(a, t):
                if a == 0 and t == 0:
                    eng.wait_ge(s_w3, 4)
                    eng.wait_ge(s_wkv, 16)
                    eng.wait_ge(s_dve0, 8)
                    for r in range(R):
                        last = mm(p_sm[:, 320:320 + W3], ones[:, :], w3[:, r, :], start=(r == 0), stop=(r == R - 1))
                    last.then_inc(s_pe0, 1)
                eng.wait_ge(s_xtc, 4 * a + 2 * t + 2)
                if a or t:
                    eng.wait_ge(s_zc, TU * a + t)
                for r in range(R):
                    last = mm(p_z[:, 0:W3], x_t[:, a % 2, r, t * P:(t + 1) * P], w3[:, r, :], start=(r == 0), stop=(r == R - 1))
                last.then_inc(s_z, 1)

            def mix(a, t):
                if t == 0:
                    if a == 0:
                        eng.wait_ge(s_mixt, 32)
                        eng.wait_ge(s_dve0, 18)
                    else:
                        eng.wait_ge(s_qkv, a)
                        eng.wait_ge(s_otc, a)
                eng.wait_ge(s_zc, TU * a + t + 1)
                for h in range(2):
                    rows = slice(h * S, h * S + S)
                    last = mm(p_sm[rows, W3 * t:W3 * t + W3], mix_t[rows, TU * a + t, :], z_sb[rows, t, :], start=True, stop=True)
                last.then_inc(s_mix, 1)

            def transpose_o(b):
                eng.wait_ge(s_o, b + 1)
                eng.wait_ge(s_qkv, b + 1)
                for t in range(TU):
                    last = eng.transpose(p_sm[:, 192 + t * P:192 + (t + 1) * P],
                                         o_rep[:, t, :, :].rearrange("p d e -> p (d e)"), ident[:, :])
                last.then_inc(s_ot, 1)

            def transpose_x1(b, g):
                if g == 0:
                    eng.wait_ge(s_x1t, b + 1)
                if b or g:
                    eng.wait_ge(s_x2l, G * b + g)
                for n in range(UB):
                    last = eng.transpose(p_x2[:, n * P:(n + 1) * P],
                                         x1_t[:, n * G + g, :, :].rearrange("p r c -> p (r c)"), ident[:, :])
                last.then_inc(s_x2, 1)

            def conv(c, g):
                if c == 0 and g == 0:
                    eng.wait_ge(s_dve0, 22)
                if c or g:
                    eng.wait_ge(s_u, G * c + g)
                eng.wait_ge(s_x2l, G * c + g + 1)
                n = 0
                for k, (hi, lo) in enumerate(((c_hi, c_lo), (y_hi, y_lo))):
                    if k == 1:
                        eng.wait_ge(s_yd[g], 32 * (c + 1))
                    for w, src in ((cw_hi, hi), (cw_hi, lo), (cw_lo, hi)):
                        last = mm(p_conv[:, :], w[:, k, g, :], runs(src, g), start=(n == 0), stop=(n == 5))
                        n += 1
                last.then_inc(s_conv, 1)

            def transpose_u(c, g):
                eng.wait_ge(s_u, G * c + g + 1)
                if c or g:
                    eng.wait_ge(s_utl, G * c + g)
                for n in range(UB):
                    last = eng.transpose(p_ut[:, n * P:(n + 1) * P], u_sb[:, g % 2, n * P:(n + 1) * P], ident[:, :])
                last.then_inc(s_ut, 1)

            def linear(d, slot):
                f, q = slot // 4, slot % 4
                t, j = f // 2, f % 2
                if q == 0:
                    if f == 0:
                        if d == 0:
                            eng.wait_ge(s_wf, 2)
                        eng.wait_ge(s_utl, G * (d + 1))
                    if d or f >= 2:
                        eng.wait_ge(s_res, 4 * d + f - 1)
                if q == 3:
                    with eng.If(inexact != 0):
                        for r in range(R):
                            for u in (u_hi, u_lo):
                                for w in (rest_hi, rest_lo):
                                    mm(p_f[f % 2][:, :], u[:, d % 2, r, t * P:(t + 1) * P],
                                       w[:, :].unsqueeze(1).broadcast_to([P, HALF // P, P]), start=False, stop=False)
                for r in (2 * q, 2 * q + 1):
                    for u in (u_hi, u_lo):
                        last = mm(p_f[f % 2][:, :], u[:, d % 2, r, t * P:(t + 1) * P], w_ffn[:, r, j * HALF:(j + 1) * HALF],
                                  start=(r == 0 and u is u_hi), stop=(r == R - 1 and u is u_lo))
                if q == 3:
                    last.then_inc(s_f, 1)

            for i in range(NI):
                a, b, c, d = i, i - 1, i - 2, i - 3
                for slot in range(SLOTS):
                    if 0 <= d < NU:
                        linear(d, slot)
                    if a < NU and slot in XT_SLOT:
                        transpose_x(a, XT_SLOT.index(slot))
                    if 0 <= c < NU and slot in UT_SLOT:
                        transpose_u(c, UT_SLOT.index(slot))
                    if 0 <= b < NU and slot in X2_SLOT:
                        transpose_x1(b, X2_SLOT.index(slot))
                    if 0 <= b < NU and slot == O_SLOT(i):
                        transpose_o(b)
                    if a < NU and slot in Z_SLOT:
                        project(a, Z_SLOT.index(slot))
                    if 0 <= c < NU and slot in CONV_SLOT:
                        conv(c, CONV_SLOT.index(slot))
                    if a < NU and slot in MIX_SLOT:
                        mix(a, MIX_SLOT.index(slot))


def kernel(**inputs):
    import numpy as np
    from concourse import bacc
    from concourse.bass_utils import run_bass_kernel_spmd

    def arr(name):
        return np.asarray(inputs[name])

    conv_w = arr("L0_cond2_weight").reshape(G, CG, CG, TAPS).transpose(2, 0, 3, 1)[:, :, ::-1, :]
    ctx_w = arr("L0_cond2_c_weight").T.reshape(P, G, 1, CG)
    arrays = {
        "x": arr("x").reshape(B * S, D),
        "cols": np.concatenate([arr("cond_128").T, arr("L0_cond_W0"), arr("L0_cond_W1"), arr("L0_cond_W2"),
                                arr("L0_cond_b0").reshape(P, 1), arr("L0_cond_b1").reshape(P, 1),
                                np.tile(arr("fside_S_0").reshape(G, CG).T, (R, 1))], axis=1),
        "row": np.concatenate([arr("L0_ffn_scale").reshape(1), arr("L0_ffn_zero_point").reshape(1), arr("L0_cond_b2"),
                               arr("L0_attn_bk").reshape(DH), arr("L0_attn_bv").reshape(DH)]).reshape(1, NROW),
        "mix_w": np.concatenate([arr("L0_cond_bias_k"), arr("L0_cond_bias_k"),
                                 arr("L0_cond_weight").reshape(KE, S, S).transpose(0, 2, 1).reshape(KE, S * S)], axis=1),
        "wq": arr("L0_attn_Wq").reshape(P, R, DH * NH), "bq": arr("L0_attn_bq").reshape(1, DH * NH),
        "wkv": np.concatenate([arr("L0_attn_Wk").reshape(P, R, DH), arr("L0_attn_Wv").reshape(P, R, DH)], axis=2),
        "conv_w": conv_w.reshape(CG, G, TAPS * CG),
        "ctx_w": np.broadcast_to(ctx_w, (P, G, R, CG)).reshape(P, G, P),
        "packed_t": arr("L0_ffn_packed_weight").T.reshape(P, R, HALF),
        "ffn_bias": arr("L0_ffn_bias").reshape(1, D),
    }
    nc = bacc.Bacc("TRN2", target_bir_lowering=False, num_devices=1)
    args = {}
    for name, a in arrays.items():
        arrays[name] = a = np.ascontiguousarray(a)
        args[name] = nc.dram_tensor(name + "_in", a.shape, mybir.dt.from_np(a.dtype), kind="ExternalInput").ap()
    args["out"] = nc.dram_tensor("out_0", (B * S, D), F32, kind="ExternalOutput").ap()
    block_program(nc, **args)
    r = run_bass_kernel_spmd(nc, [{name + "_in": a for name, a in arrays.items()}], core_ids=[0])
    return r.results[0]["out_0"].reshape(B, S, D)
```

```python
import concourse.bass as bass
from concourse import mybir
from contextlib import ExitStack

F32 = mybir.dt.float32
F32R = mybir.dt.float32r
I32 = mybir.dt.int32
U8 = mybir.dt.uint8
ALU = mybir.AluOpType
ACT = mybir.ActivationFunctionType
AX = mybir.AxisListType

P = 128
B, S, D = 64, 64, 1024
DH, NH = 32, 32
KE = 8
R = D // P
G, CG = 4, 16
TAPS, PAD = 9, 4
UB = 4
TU = 2
UT = UB * S
NU = B // UB
NT = NU * TU
SLOTS = 16
W3 = 3 * DH
COLS = 1 + G * UB * (P + 1)
HALF = D // 2
ZLIM = 1000.0
NX = 5


COLS_AT = {"cond": (0, B), "w0": (B, P), "w1": (B + P, P), "w2": (B + 2 * P, KE), "b0": (B + 2 * P + KE, 1),
           "b1": (B + 2 * P + KE + 1, 1), "cbias": (B + 2 * P + KE + 2, G), "part": (B + 2 * P + KE + 2 + G, 1)}
NCOLS = B + 2 * P + KE + 3 + G
ROW_AT = {"scale": 0, "zero": 1, "b2": 2, "bk": 2 + KE, "bv": 2 + KE + DH}
NROW = 2 + KE + 2 * DH


def block_program(nc, x, cols, row, mix_w, wq, bq, wkv, conv_w, ctx_w, packed_t, ffn_bias, out):
    ctx = ExitStack()
    with ctx:
        def sb(name, shape, dt=F32):
            return ctx.enter_context(nc.sbuf_tensor(name, shape, dt))

        def ps(name):
            return ctx.enter_context(nc.psum_tensor(name, [P, 512], F32))

        def sem(name):
            return ctx.enter_context(nc.semaphore(name))

        x_nat = sb("x_nat", [P, NX, TU, D])
        x_t = sb("x_t", [P, TU, R, P])
        x1_p = sb("x1_p", [P, TU, R, P])
        x_c = sb("x_c", [P, UB * G, P])
        w3 = sb("w3", [P, R, W3])
        z_sb = sb("z_sb", [P, TU, W3])
        qkv_bias = sb("qkv_bias", [P, TU, W3])
        qkv = sb("qkv", [P, TU, W3])
        prob = sb("prob", [P, TU, DH, DH])
        k_max = sb("k_max", [P, TU])
        k_min = sb("k_min", [P, TU])
        top = sb("top", [P, TU, DH])
        top2 = sb("top2", [P, TU, DH])
        den = sb("den", [P, TU, DH])
        rden = sb("rden", [P, TU, DH])
        num = sb("num", [P, TU, DH])
        o_sb = sb("o_sb", [P, TU, DH])
        c_in = sb("c_in", [P, 2, COLS], F32R)
        y_in = sb("y_in", [P, 2, COLS], F32R)
        c_hi, c_lo, y_hi, y_lo = c_in[:, 0, :], c_in[:, 1, :], y_in[:, 0, :], y_in[:, 1, :]
        u_sb = sb("u_sb", [P, 2, UB * P])
        u_hi = sb("u_hi", [P, 2, R, UT], F32R)
        u_lo = sb("u_lo", [P, 2, R, UT], F32R)
        w_ffn = sb("w_ffn", [P, R, D], F32R)
        cw_hi = sb("cw_hi", [P, 2, G, P], F32R)
        cw_lo = sb("cw_lo", [P, 2, G, P], F32R)
        mix_t = sb("mix_t", [P, NT, S])
        ffn_b = sb("ffn_b", [P, D])
        rest_hi = sb("rest_hi", [P, P], F32R)
        rest_lo = sb("rest_lo", [P, P], F32R)
        ident = sb("ident", [P, P])
        ones = sb("ones", [P, P])
        cols_sb = sb("cols_sb", [P, NCOLS])
        row_sb = sb("row_sb", [P, NROW])
        cond_sb, w0_sb, w1_sb, w2_sb, b0_sb, b1_sb, cbias_sb, part_sb = (
            cols_sb[:, at:at + n] for at, n in COLS_AT.values())
        sc = row_sb[:, 0:1]
        b2_sb = row_sb[0:B, ROW_AT["b2"]:ROW_AT["b2"] + KE]
        h_sb = sb("h_sb", [P, 2, B])
        att = sb("att", [B, 4, KE])
        att_s = sb("att_s", [B, 4])
        att_r = sb("att_r", [B, 3 * KE], F32R)
        att_t = sb("att_t", [3 * KE, B], F32R)
        mix_bias = sb("mix_bias", [P, NT])
        u_bias = sb("u_bias", [P, G, B])
        zp = sb("zp", [P, 5])
        zi = sb("zi", [P, 1], I32)
        flag = sb("flag", [1, 2], I32)
        bias3 = sb("bias3", [P, W3])
        col3 = sb("col3", [P, W3])
        cw = u_sb[:, :, :].rearrange("p y (g n) -> p y g n", g=G)
        def halves(t, rows):
            return t[rows, :, :, :].rearrange("p a b c -> p (a b c)")

        ew = slice(0, 3 * KE)
        mixw = halves(prob, ew), halves(x1_p, ew)
        mixw_hi = (u_hi[ew, 0, :, :].rearrange("k r t -> k (r t)"), u_hi[ew, 1, :, :].rearrange("k r t -> k (r t)"))
        mixw_r = (u_lo[ew, 0, :, :].rearrange("k r t -> k (r t)"), u_lo[ew, 1, :, :].rearrange("k r t -> k (r t)"))
        mixed = halves(prob, slice(0, B)), halves(x1_p, slice(0, B))
        packed = x_c[:, G:3 * G, :].rearrange("p n m -> p (n m)").bitcast(U8).rearrange("p (r n) -> p r n", n=HALF)
        low4 = x_nat[:, 4, 0, :].bitcast(U8).rearrange("p (r n) -> p r n", n=HALF)
        ctx_sb = x_c[:, 0:G, :]
        bq_tmp = ffn_b[:, :].rearrange("p (d h) -> p d h", h=NH)
        mixb_sb = qkv[0:2 * KE, :, :].rearrange("k t w -> k (t w)")[:, 0:P]

        p_z, p_sm, p_conv, p_ut = (ps(n) for n in ("p_z", "p_sm", "p_conv", "p_ut"))
        p_xt = [ps("p_xt0"), ps("p_xt1")]
        p_f = [ps("p_f0"), ps("p_f1")]
        p_mixed = [p_f[0], p_f[1], p_ut, p_z]

        mixed_dram = nc.dram_tensor("mixed_dram", [B, S * S], F32).ap()
        x1_dram = nc.dram_tensor("x1_dram", [B * S, R, P], F32).ap()

        s_small = sem("s_small")
        s_small2 = sem("s_small2")
        s_wq = [sem(f"s_wq{i}") for i in range(4)]
        s_wkv = sem("s_wkv")
        s_mw = [sem(f"s_mw{j}") for j in range(2)]
        s_pk = sem("s_pk")
        s_cw = sem("s_cw")
        s_x = [sem(f"s_xload{i}") for i in range(NX)]
        s_out = [sem(f"s_out{i}") for i in range(NX)]
        s_yd = [sem(f"s_yd{g}") for g in range(G)]
        s_pool0 = sem("s_pool0")
        s_pe0 = sem("s_pe0")
        s_act0 = sem("s_act0")
        s_mwh = sem("s_mwh")
        s_mwr = sem("s_mwr")
        s_att = sem("s_att")
        s_mixb = sem("s_mixb")
        s_zp = sem("s_zp")
        s_flag = sem("s_flag")
        s_rest = sem("s_rest")
        s_nib = sem("s_nib")
        s_col = sem("s_col")
        s_ub = sem("s_ub")
        s_mixed = sem("s_mixed")
        s_mixedc = sem("s_mixedc")
        s_mixedd = [sem(f"s_mixedd{n}") for n in range(2)]
        s_mixt = [sem(f"s_mixt{n}") for n in range(2)]
        s_bq = sem("s_bq")
        s_bqr = sem("s_bqr")
        s_ffb = sem("s_ffb")
        s_w3 = sem("s_w3")
        s_wf = sem("s_wf")
        s_xt = sem("s_xt")
        s_xtc = sem("s_xtc")
        s_z = sem("s_z")
        s_zc = sem("s_zc")
        s_mix = sem("s_mix")
        s_qb = sem("s_qb")
        s_qkv = sem("s_qkv")
        s_top = sem("s_top")
        s_score = sem("s_score")
        s_sub = sem("s_sub")
        s_exp = sem("s_exp")
        s_den = sem("s_den")
        s_pv = sem("s_pv")
        s_num = sem("s_num")
        s_rden = sem("s_rden")
        s_o = sem("s_o")
        s_x1 = sem("s_x1")
        s_x1p = sem("s_x1p")
        s_xb = sem("s_xb")
        s_x1s = [sem(f"s_x1s{t}") for t in range(TU)]
        s_xc = sem("s_xc")
        s_x2h = sem("s_x2h")
        s_x2l = sem("s_x2l")
        s_conv = sem("s_conv")
        s_u = sem("s_u")
        s_ut = sem("s_ut")
        s_uth = sem("s_uth")
        s_utl = sem("s_utl")
        s_f = sem("s_f")
        s_res = sem("s_res")

        block = ctx.enter_context(nc.Block())

        def xbuf(u):
            return x_nat[:, u % NX, :, :]

        def col(g, n):
            return 1 + (g * UB + n) * (P + 1)

        def runs(t, g):
            return t[:, col(g, 0):col(g, 0) + UB * (P + 1)].rearrange("p (n c) -> p n c", c=P + 1)[:, :, 0:P]

        def ut_view(t, u, g):
            v = t[:, u % 2, :, :].rearrange("p r (n c) -> p n r c", n=UB)
            return v[:, :, :, g * CG:(g + 1) * CG]

        N_SMALL, N_SMALL2 = 3, 1
        N_CW = 2 * R
        NI = NU + 4

        XT_SLOT = (0, 1, 2, 3)
        Z_SLOT = (4, 7)
        MIX_SLOT = (7, 8)
        TOP_SLOT = 7
        SCORE_SLOT = (9, 10)
        SUB_SLOT = (10, 12)
        EXP_SLOT = (11, 13)
        DEN_SLOT = (12, 13)
        PV_SLOT = (13, 15)
        NUM_SLOT = (16, 17)
        O_SLOT = (16, 17)
        X1_SLOT = (1, 4)
        X1P_SLOT = (2, 4)
        XC_SLOT = 6
        X2_SLOT = (10, 11, 13, 14)
        BIAS_SLOT = 5
        CONV_SLOT = (0, 2, 6, 9)
        UT_SLOT = (2, 5, 8, 11)
        FINISH_SLOT = (4, 9, 11)

        CONVERT_SLOT = (5, 14)
        AHEAD = 9
        XT_AHEAD = (9, 10, 12, 13)
        Z_AHEAD = (13, 15)
        EXP0_SLOT = (8, 11)
        X20_SLOT = (12, 13, 14, 15)
        X1P1_SLOT = (0, 1)
        XC1_SLOT = 2
        MIX2_SLOT = (0, 1)
        TOP2_SLOT = 1
        SCORE2_SLOT = (1, 2)
        SUB2_SLOT = (1, 2)
        EXP2_SLOT = (3, 4)
        CONV0_SLOT = (1, 2, 3, 4)
        UT0_SLOT = (2, 4, 5, 6)

        def conv_bank(c, g):
            return p_f[0] if c == 0 and g % 2 else p_conv

        def x1p_slots(b):
            return X1P1_SLOT if b == 1 else X1P_SLOT

        def mix_slots(a):
            return MIX2_SLOT if a == 2 else MIX_SLOT

        def x2_slots(b):
            return X20_SLOT if b == 0 else X2_SLOT

        def stage_a(i, slot):
            if slot >= AHEAD:
                return (i + 1, XT_AHEAD, Z_AHEAD) if i < 2 else (i, (), ())
            return (i, (), ()) if i in (1, 2) or i >= NU else (i, XT_SLOT, Z_SLOT)

        def stage_c(c):
            return ((), ()) if not 0 <= c < NU else (CONV0_SLOT, UT0_SLOT) if c == 0 else (CONV_SLOT, UT_SLOT)

        @block.sync
        def _(eng):
            def load_x(u):
                if u >= NX:
                    eng.wait_ge(s_out[u % NX], 32 * (u // NX))
                for t in range(TU):
                    row = (u * TU + t) * P
                    eng.dma_start(x_nat[:, u % NX, t, :], x[row:row + P, :]).then_inc(s_x[u % NX], 16)

            def load_first(u):
                eng.wait_ge(s_w3, u)
                load_x(u)

            def store(d, t):
                eng.wait_ge(s_res, 4 * d + 2 * t + 2)
                row = (d * TU + t) * P
                eng.dma_start(out[row:row + P, :], x_nat[:, d % NX, t, :]).then_inc(s_out[d % NX], 16)

            eng.dma_start(cols_sb[:, :], cols).then_inc(s_small, 16)
            eng.dma_start(row_sb[:, :], row.broadcast_to([P, NROW])).then_inc(s_small, 16)
            for j in range(2):
                eng.dma_start(mixw[j], mix_w[:, P + 2048 * j:P + 2048 * j + 2048]).then_inc(s_mw[j], 16)
            eng.dma_start(mixb_sb, mix_w[0:2 * KE, 0:P]).then_inc(s_small, 16)
            load_x(0)
            for c in range(4):
                eng.dma_start(x_nat[:, 1 + c, :, :], wq[:, 2 * c:2 * c + 2, :]).then_inc(s_wq[c], 16)
            parts = (0, B // 4), (B // 4, B)
            for j in range(2):
                eng.wait_ge(s_mixedc, 4 * (j + 1))
                b0, b1 = parts[0]
                eng.dma_start(mixed_dram[b0:b1, 2048 * j:2048 * j + 2048], mixed[j][b0:b1, :]).then_inc(s_mixedd[0], 16)
            b0, b1 = parts[1]
            for j in range(2):
                eng.dma_start(mixed_dram[b0:b1, 2048 * j:2048 * j + 2048], mixed[j][b0:b1, :]).then_inc(s_mixedd[1], 16)
            for n, (b0, b1) in enumerate(parts):
                eng.wait_ge(s_mixedd[n], 32)
                for h in range(2):
                    eng.dma_start(mix_t[h * S:h * S + S, b0 // 2:b1 // 2, :],
                                  mixed_dram[b0:b1, :].rearrange("(t h) (i s) -> h i t s", h=2, i=S)[h]).then_inc(s_mixt[n], 16)
                if n == 0:
                    load_first(1)
            load_first(2)
            eng.wait_ge(s_bqr, 1)
            eng.dma_start(ffn_b[:, :], ffn_bias.broadcast_to([P, D])).then_inc(s_ffb, 16)

            for i in range(NI):
                a, b, d = i, i - 1, i - 3
                for slot in range(SLOTS):
                    if slot == 2 and 0 <= d - 1 < NU:
                        store(d - 1, 1)
                    if slot == 2 and a >= 1 and 3 <= a + 1 < NU:
                        if a + 1 < NX:
                            eng.wait_ge(s_w3, a + 1)
                        if a + 1 == NX - 1:
                            eng.wait_ge(s_wf, 1)
                        load_x(a + 1)
                    if 0 <= b < NU and slot in x1p_slots(b):
                        t = x1p_slots(b).index(slot)
                        eng.wait_ge(s_x1p, TU * b + t + 1)
                        at = (b * TU + t) * P
                        eng.dma_start(x1_dram[at:at + P], x1_p[:, t, :, :]).then_inc(s_x1s[t], 16)
                    if 0 <= b < NU and slot == (XC1_SLOT if b == 1 else XC_SLOT):
                        for t in range(TU):
                            eng.wait_ge(s_x1s[t], 16 * (b + 1))
                        if b == 0:
                            eng.wait_ge(s_ub, 1)
                            eng.wait_ge(s_wf, 2)
                        if b:
                            eng.wait_ge(s_x2l, G * b)
                        for r in range(R):
                            eng.dma_start(x_c[r * CG:(r + 1) * CG, :, :],
                                          x1_dram[b * UT:(b + 1) * UT, r, :].rearrange("(n c) m -> c n m", c=CG)).then_inc(s_xc, 16)
                    if 0 <= b < NU and slot in x2_slots(b):
                        g = x2_slots(b).index(slot)
                        eng.wait_ge(s_x2h, G * b + g + 1)
                        eng.wait_ge(s_x2l, G * b + g + 1)
                        if b:
                            eng.wait_ge(s_conv, G * (b - 1) + g + 1)
                        c0, n = col(g, 0), UB * (P + 1) - 1
                        src, dst = c_in[:, :, :].bitcast(F32), y_in[:, :, :].bitcast(F32)
                        eng.dma_start(dst[0:64, :, c0:c0 + n], src[0:64, :, c0 + 1:c0 + 1 + n]).then_inc(s_yd[g], 16)
                        eng.dma_start(dst[64:P, :, c0:c0 + n], src[64:P, :, c0 - 1:c0 - 1 + n]).then_inc(s_yd[g], 16)
                    if 0 <= d < NU and slot == 9:
                        store(d, 0)
            for k in range(NX):
                eng.wait_ge(s_out[k], 32 * len(range(k, NU, NX)))

        @block.gpsimd
        def _(eng):
            eng.memset(ident[:, :], 0.0).then_inc(s_pool0, 1)
            eng.memset(u_sb[:, :, :], 0.0).then_inc(s_pool0, 1)
            eng.memset(ones[:, :], 1.0).then_inc(s_pool0, 1)
            eng.wait_ge(s_pool0, 3)
            eng.affine_select(out=ident[:, :], in_=ident[:, :], compare_op=ALU.not_equal, fill=1.0,
                              base=0, pattern=[[-1, P]], channel_multiplier=1).then_inc(s_pool0, 1)
            for t in (c_in, y_in):
                eng.memset(t[:, :, 0:COLS:P + 1].bitcast(F32), 0.0).then_inc(s_pool0, 1)
            for r in range(R):
                lo, hi = max(0, r - PAD), min(R - 1, r + PAD)
                eng.dma_start(cw[r * CG:(r + 1) * CG, 0, :, lo * CG:(hi + 1) * CG],
                              conv_w[:, :, (lo - r + PAD) * CG:(hi - r + PAD + 1) * CG]).then_inc(s_cw, 16)
                lo, hi, k = (r + PAD, R - 1, 0) if r < PAD else (0, r - PAD, 12 - r)
                eng.dma_start(cw[r * CG:(r + 1) * CG, 1, :, lo * CG:(hi + 1) * CG],
                              conv_w[:, :, k * CG:(k + hi - lo + 1) * CG]).then_inc(s_cw, 16)

            eng.wait_ge(s_cw, 16 * N_CW)
            eng.tensor_copy(cw_hi[:, :, :, :], cw).then_inc(s_pool0, 1)
            eng.wait_ge(s_pool0, 7)
            eng.tensor_tensor(cw_lo[:, :, :, :], cw, cw_hi[:, :, :, :].bitcast(F32), ALU.subtract).then_inc(s_pool0, 1)

            for i in range(NI):
                b = i - 1
                for slot in range(SLOTS):
                    if 0 <= b < NU and slot in X1_SLOT:
                        t = X1_SLOT.index(slot)
                        eng.wait_ge(s_o, TU * b + t + 1)
                        xv = xbuf(b)[:, t, :].rearrange("p (d h) -> p d h", h=NH)
                        eng.tensor_tensor(xv, xv, o_sb[:, t, :].unsqueeze(2).broadcast_to([P, DH, NH]), ALU.add).then_inc(s_x1, 1)
                    if 0 <= b < NU and slot == BIAS_SLOT:
                        if b == 0:
                            eng.wait_ge(s_ffb, 16)
                        eng.wait_ge(s_x1p, TU * (b + 1))
                        eng.tensor_tensor(xbuf(b), xbuf(b), ffn_b[:, :].unsqueeze(1).broadcast_to([P, TU, D]), ALU.add).then_inc(s_xb, 1)
                    if 0 <= b < NU and slot in x2_slots(b):
                        g = x2_slots(b).index(slot)
                        eng.wait_ge(s_x2h, G * b + g + 1)
                        eng.tensor_tensor(runs(c_lo, g), x_c[:, g::G, :], runs(c_hi, g).bitcast(F32), ALU.subtract).then_inc(s_x2l, 1)

        @block.scalar
        def _(eng):
            for n, bias in enumerate((b0_sb, b1_sb)):
                eng.wait_ge(s_pe0, n + 1)
                eng.activation(h_sb[:, n, :], p_sm[:, 64 * n:64 * n + 64], ACT.Gelu, bias=bias).then_inc(s_act0, 1)
            eng.wait_ge(s_att, 3)
            eng.activation(att[:, 1, :], att[:, 0, :], ACT.Exp, accum_out=att_s[:, 2:3]).then_inc(s_act0, 1)
            eng.dma_start(w3[:, :, DH:W3], wkv).then_inc(s_wkv, 16)
            eng.dma_start(bq_tmp, bq.broadcast_to([P, DH * NH]).rearrange("p (d h) -> p d h", h=NH)).then_inc(s_bq, 16)
            for c in range(8):
                eng.wait_ge(s_mixed, c + 1)
                eng.activation(mixed[c // 4][:, 512 * (c % 4):512 * (c % 4) + 512], p_mixed[c % 4][0:B, :], ACT.Copy).then_inc(s_mixedc, 1)

            eng.dma_start(packed, packed_t).then_inc(s_pk, 16)
            eng.dma_start(ctx_sb, ctx_w).then_inc(s_small2, 16)

            def convert_weights(half):
                eng.wait_ge(s_nib, half + 1)
                eng.activation(w_ffn[:, :, half:D:2], (low4, packed)[half], ACT.Identity, bias=zp[:, 4:5]).then_inc(s_wf, 1)

            def xt_copy(a, k):
                eng.wait_ge(s_xt, 4 * a + k + 1)
                t, r0 = k // 2, 4 * (k % 2)
                if a and k % 2 == 0:
                    eng.wait_ge(s_z, TU * (a - 1) + t + 1)
                eng.activation(x_t[:, t, r0:r0 + 4, :], p_xt[k % 2][:, :].rearrange("p (r t) -> p r t", t=P), ACT.Copy).then_inc(s_xtc, 1)

            def z_copy(a, t):
                eng.wait_ge(s_z, TU * a + t + 1)
                if a:
                    eng.wait_ge(s_mix, TU * (a - 1) + t + 1)
                eng.activation(z_sb[:, t, :], p_z[:, 0:W3], ACT.Copy).then_inc(s_zc, 1)

            def x1_permute(b, t):
                eng.wait_ge(s_x1, TU * b + t + 1)
                if b:
                    eng.wait_ge(s_x1s[t], 16 * b)
                eng.activation(x1_p[:, t, :, :], xbuf(b)[:, t, :].rearrange("p (m r) -> p r m", r=R), ACT.Copy).then_inc(s_x1p, 1)

            def x2_hi(b, g):
                eng.wait_ge(s_xc, 16 * R * (b + 1))
                if b:
                    eng.wait_ge(s_conv, G * (b - 1) + g + 1)
                eng.activation(runs(c_hi, g), x_c[:, g::G, :], ACT.Copy).then_inc(s_x2h, 1)

            def ut_hi(c, g):
                eng.wait_ge(s_ut, G * c + g + 1)
                if c >= 2:
                    eng.wait_ge(s_f, 4 * (c - 1))
                eng.activation(ut_view(u_hi, c, g),
                               p_ut[:, :].rearrange("p (n r c) -> p n r c", n=UB, r=R), ACT.Copy).then_inc(s_uth, 1)

            def u_copy(c, g):
                eng.wait_ge(s_conv, G * c + g + 1)
                if c or g >= 2:
                    eng.wait_ge(s_ut, G * c + g - 1)
                elif g == 0:
                    eng.wait_ge(s_ub, 1)
                for n in range(UB):
                    ins = eng.activation(u_sb[:, g % 2, n * P:(n + 1) * P], conv_bank(c, g)[:, n * P:(n + 1) * P], ACT.Identity,
                                         bias=u_bias[:, g, UB * c + n:UB * c + n + 1], scale=sc)
                ins.then_inc(s_u, 1)

            for i in range(NI):
                a, b, c = i, i - 1, i - 2
                for slot in range(SLOTS):
                    (xa, xt_slots, z_slots), (conv_slots, ut_slots) = stage_a(i, slot), stage_c(c)
                    if slot in conv_slots:
                        u_copy(c, conv_slots.index(slot))
                    if slot in xt_slots:
                        xt_copy(xa, xt_slots.index(slot))
                    if slot in ut_slots:
                        ut_hi(c, ut_slots.index(slot))
                    if 0 <= b < NU and slot in x2_slots(b):
                        x2_hi(b, x2_slots(b).index(slot))
                    if 0 <= b < NU and slot in x1p_slots(b):
                        x1_permute(b, x1p_slots(b).index(slot))
                    if slot in z_slots:
                        z_copy(xa, z_slots.index(slot))
                    exp_slots = EXP_SLOT if a > 2 else EXP2_SLOT if a == 2 else EXP0_SLOT
                    if a < NU and slot in exp_slots:
                        t = exp_slots.index(slot)
                        eng.wait_ge(s_sub, TU * a + t + 1)
                        flat = prob[:, t, :, :].rearrange("p d e -> p (d e)")
                        eng.activation(flat, flat, ACT.Exp, scale=float(DH) ** -0.5).then_inc(s_exp, 1)
                    if i == 0 and slot in CONVERT_SLOT:
                        convert_weights(CONVERT_SLOT.index(slot))

        @block.vector
        def _(eng):
            def chunk_sum(c):
                eng.wait_ge(s_wq[c], 16)
                eng.tensor_reduce(w3[:, 2 * c:2 * c + 2, 0:DH],
                                  x_nat[:, 1 + c, :, :].rearrange("p t (d h) -> p t d h", h=NH), AX.X, ALU.add).then_inc(s_w3, 1)

            for j in range(2):
                eng.wait_ge(s_mw[j], 16)
                eng.tensor_copy(mixw_hi[j], mixw[j]).then_inc(s_mwh, 1)
            eng.wait_ge(s_small, 16 * N_SMALL)
            for j in range(2):
                eng.wait_ge(s_mwh, j + 1)
                eng.scalar_tensor_tensor(out=mixw_r[j], in0=mixw_hi[j].bitcast(F32), scalar=part_sb[ew, :], in1=mixw[j],
                                         op0=ALU.mult, op1=ALU.add).then_inc(s_mwr, 1)
            eng.wait_ge(s_pe0, 3)
            eng.tensor_tensor(att[:, 0, :], p_sm[0:B, 128:128 + KE], b2_sb, ALU.add).then_inc(s_att, 1)
            eng.wait_ge(s_att, 1)
            eng.tensor_reduce(att_s[:, 0:1], att[:, 0, :], AX.X, ALU.max).then_inc(s_att, 1)
            eng.wait_ge(s_att, 2)
            eng.tensor_scalar(att[:, 0, :], att[:, 0, :], att_s[:, 0:1], None, ALU.subtract).then_inc(s_att, 1)
            eng.wait_ge(s_act0, 3)
            eng.reciprocal(att_s[:, 3:4], att_s[:, 2:3]).then_inc(s_att, 1)
            eng.wait_ge(s_att, 4)
            eng.tensor_scalar(att[:, 2, :], att[:, 1, :], att_s[:, 3:4], None, ALU.mult).then_inc(s_att, 1)
            eng.wait_ge(s_att, 5)
            for n in (0, 2):
                eng.tensor_copy(att_r[:, n * KE:n * KE + KE], att[:, 2, :]).then_inc(s_att, 1)
            eng.wait_ge(s_att, 6)
            eng.tensor_tensor(att_r[:, KE:2 * KE], att[:, 2, :], att_r[:, 0:KE].bitcast(F32), ALU.subtract).then_inc(s_att, 1)
            eng.wait_ge(s_pe0, 4)
            eng.tensor_copy(att_t[:, :], p_sm[0:3 * KE, 192:192 + B]).then_inc(s_att, 1)
            eng.wait_ge(s_pe0, 5)
            for h in range(2):
                eng.tensor_copy(mix_bias[h * S:h * S + S, :], p_sm[h * S:h * S + S, 256 + h:256 + B:2]).then_inc(s_mixb, 1)
            zero = row_sb[:, ROW_AT["zero"]:ROW_AT["zero"] + 1]
            eng.tensor_scalar(zp[:, 1:2], zero, ZLIM, -ZLIM, ALU.min, ALU.max).then_inc(s_zp, 1)
            eng.wait_ge(s_zp, 1)
            eng.tensor_copy(zi[:, :], zp[:, 1:2]).then_inc(s_zp, 1)
            eng.wait_ge(s_zp, 2)
            eng.tensor_copy(zp[:, 2:3], zi[:, :]).then_inc(s_zp, 1)
            eng.wait_ge(s_zp, 3)
            eng.tensor_tensor(zp[:, 3:4], zp[:, 2:3], zero, ALU.subtract).then_inc(s_zp, 1)
            eng.tensor_scalar(zp[:, 4:5], zp[:, 2:3], -1.0, None, ALU.mult).then_inc(s_zp, 1)
            eng.wait_ge(s_zp, 4)
            rest = zp[:, 3:4].broadcast_to([P, P])
            eng.tensor_scalar(flag[0:1, 0:1], zp[0:1, 3:4], 0.0, None, ALU.not_equal).then_inc(s_flag, 1)
            eng.tensor_copy(rest_hi[:, :], rest).then_inc(s_rest, 1)
            eng.wait_ge(s_rest, 1)
            eng.tensor_tensor(rest_lo[:, :], rest, rest_hi[:, :].bitcast(F32), ALU.subtract).then_inc(s_rest, 1)
            for c in range(4):
                chunk_sum(c)
            eng.wait_ge(s_bq, 16)
            eng.tensor_reduce(bias3[:, 0:DH], bq_tmp, AX.X, ALU.add).then_inc(s_bqr, 1)
            eng.tensor_copy(bias3[:, DH:W3], row_sb[:, ROW_AT["bk"]:ROW_AT["bk"] + 2 * DH]).then_inc(s_bqr, 1)
            eng.wait_ge(s_pk, 16)
            eng.wait_ge(s_w3, 4)
            eng.tensor_scalar(low4, packed, 15, None, ALU.bitwise_and).then_inc(s_nib, 1)
            eng.wait_ge(s_nib, 1)
            eng.tensor_scalar(packed, packed, 4, None, ALU.logical_shift_right).then_inc(s_nib, 1)
            eng.wait_ge(s_pe0, 6)
            eng.tensor_copy(col3[:, :], p_sm[:, 320:320 + W3]).then_inc(s_col, 1)

            def bias_of_u():
                eng.wait_ge(s_pe0, 7)
                for g in range(G):
                    ins = eng.tensor_scalar(u_bias[:, g, :], p_conv[:, B * g:B * g + B], cbias_sb[:, g:g + 1], sc, ALU.add, ALU.mult)
                ins.then_inc(s_ub, 1)

            def softmax_top(a):
                q, k = qkv[:, :, 0:DH], qkv[:, :, DH:2 * DH]
                eng.wait_ge(s_qkv, a + 1)
                for dst, op in ((k_max, ALU.max), (k_min, ALU.min)):
                    eng.tensor_reduce(dst[:, :], k, AX.X, op).then_inc(s_top, 1)
                for n, (dst, src) in enumerate(((top, k_max), (top2, k_min))):
                    eng.wait_ge(s_top, 5 * a + n + 1)
                    eng.tensor_tensor(dst[:, :, :], q, src[:, :].unsqueeze(2).broadcast_to([P, TU, DH]), ALU.mult).then_inc(s_top, 1)
                eng.wait_ge(s_top, 5 * a + 4)
                eng.tensor_tensor(top[:, :, :], top[:, :, :], top2[:, :, :], ALU.max).then_inc(s_top, 1)

            def down(v):
                return v.unsqueeze(2).broadcast_to([P, DH, DH])

            def along(v):
                return v.unsqueeze(1).broadcast_to([P, DH, DH])

            def score(a, t):
                if a == 0:
                    eng.wait_ge(s_mixedd[1], 32)
                eng.tensor_tensor(prob[:, t, :, :], down(qkv[:, t, 0:DH]), along(qkv[:, t, DH:2 * DH]), ALU.mult).then_inc(s_score, 1)

            def subtract(a, t):
                eng.wait_ge(s_score, TU * a + t + 1)
                eng.wait_ge(s_top, 5 * a + 5)
                eng.tensor_tensor(prob[:, t, :, :], prob[:, t, :, :], down(top[:, t, :]), ALU.subtract).then_inc(s_sub, 1)

            def sum_exp(a, t):
                eng.wait_ge(s_exp, TU * a + t + 1)
                eng.tensor_reduce(den[:, t, :], prob[:, t, :, :], AX.X, ALU.add).then_inc(s_den, 1)

            def times_v(a, t):
                eng.wait_ge(s_den, TU * a + t + 1)
                eng.tensor_tensor(prob[:, t, :, :], prob[:, t, :, :], along(qkv[:, t, 2 * DH:]), ALU.mult).then_inc(s_pv, 1)

            def sum_v(b, t):
                eng.wait_ge(s_pv, TU * b + t + 1)
                eng.tensor_reduce(num[:, t, :], prob[:, t, :, :], AX.X, ALU.add).then_inc(s_num, 1)

            def divide(b, t):
                eng.wait_ge(s_den, TU * b + t + 1)
                eng.reciprocal(rden[:, t, :], den[:, t, :]).then_inc(s_rden, 1)
                eng.wait_ge(s_num, TU * b + t + 1)
                eng.wait_ge(s_rden, TU * b + t + 1)
                if b:
                    eng.wait_ge(s_x1, TU * (b - 1) + t + 1)
                eng.tensor_tensor(o_sb[:, t, :], num[:, t, :], rden[:, t, :], ALU.mult).then_inc(s_o, 1)

            def finish(d, f):
                t, j = f // 2, f % 2
                eng.wait_ge(s_f, 4 * d + f + 1)
                if f == 0:
                    eng.wait_ge(s_xb, d + 1)
                part = x_nat[:, d % NX, t, j * HALF:(j + 1) * HALF]
                eng.tensor_tensor(part, p_f[f % 2][:, :], part, ALU.add).then_inc(s_res, 1)

            for i in range(NI):
                a, b, c, d = i, i - 1, i - 2, i - 3
                for slot in range(SLOTS):
                    if slot == 0 and 0 <= d - 1 < NU:
                        finish(d - 1, 3)
                    if slot in FINISH_SLOT and 0 <= d < NU:
                        finish(d, FINISH_SLOT.index(slot))
                    ut_slots = stage_c(c)[1]
                    if slot in ut_slots:
                        g = ut_slots.index(slot)
                        eng.wait_ge(s_uth, G * c + g + 1)
                        eng.tensor_tensor(ut_view(u_lo, c, g), p_ut[:, :].rearrange("p (n r c) -> p n r c", n=UB, r=R),
                                          ut_view(u_hi, c, g).bitcast(F32), ALU.subtract).then_inc(s_utl, 1)
                    for u, at in ((a, slot), (b, slot + SLOTS)):
                        if 0 <= u < NU and at in NUM_SLOT:
                            sum_v(u, NUM_SLOT.index(at))
                        if 0 <= u < NU and at in O_SLOT:
                            divide(u, O_SLOT.index(at))
                    if a < NU and slot == (TOP2_SLOT if a == 2 else TOP_SLOT):
                        if a == 0:
                            eng.wait_ge(s_col, 1)
                            eng.wait_ge(s_bqr, 2)
                        for t in range(TU):
                            eng.scalar_tensor_tensor(out=qkv_bias[:, t, :], in0=col3[:, :], scalar=mix_bias[:, TU * a + t:TU * a + t + 1],
                                                     in1=bias3[:, :], op0=ALU.mult, op1=ALU.add).then_inc(s_qb, 1)
                        eng.wait_ge(s_qb, TU * (a + 1))
                        eng.wait_ge(s_mix, TU * (a + 1))
                        eng.tensor_tensor(qkv[:, :, :], p_sm[:, 0:TU * W3].rearrange("p (t w) -> p t w", t=TU),
                                          qkv_bias[:, :, :], ALU.add).then_inc(s_qkv, 1)
                        softmax_top(a)
                    if a < NU:
                        for at, what in ((SCORE2_SLOT if a == 2 else SCORE_SLOT, score), (SUB2_SLOT if a == 2 else SUB_SLOT, subtract),
                                         (DEN_SLOT, sum_exp), (PV_SLOT, times_v)):
                            if slot in at:
                                what(a, at.index(slot))
                    if i == 0 and slot == SLOTS - 1:
                        bias_of_u()

        @block.tensor
        def _(eng):
            mm = eng.matmul
            def transpose_x(a, k):
                if k == 0:
                    eng.wait_ge(s_x[a % NX], 32 * (a // NX + 1))
                if a or k >= 2:
                    eng.wait_ge(s_xtc, 4 * a + k - 1)
                t, r0 = k // 2, 4 * (k % 2)
                for r in range(4):
                    last = eng.transpose(p_xt[k % 2][:, r * P:(r + 1) * P], x_nat[:, a % NX, t, r0 + r:D:R], ident[:, :])
                last.then_inc(s_xt, 1)

            def project(a, t):
                if a == 0 and t == 0:
                    eng.wait_ge(s_w3, 4)
                    eng.wait_ge(s_wkv, 16)
                eng.wait_ge(s_xtc, 4 * a + 2 * t + 2)
                if a or t:
                    eng.wait_ge(s_zc, TU * a + t)
                else:
                    eng.wait_ge(s_mixedc, 8)
                for r in range(R):
                    last = mm(p_z[:, 0:W3], x_t[:, t, r, :], w3[:, r, :], start=(r == 0), stop=(r == R - 1))
                last.then_inc(s_z, 1)

            def mix(a, t):
                if t == 0:
                    if a == 0:
                        eng.wait_ge(s_mixt[0], 32)
                        eng.wait_ge(s_col, 1)
                    else:
                        eng.wait_ge(s_qkv, a)
                if a == NU // 4 and t == 0:
                    eng.wait_ge(s_mixt[1], 32)
                eng.wait_ge(s_zc, TU * a + t + 1)
                for h in range(2):
                    rows = slice(h * S, h * S + S)
                    last = mm(p_sm[rows, W3 * t:W3 * t + W3], mix_t[rows, TU * a + t, :], z_sb[rows, t, :], start=True, stop=True)
                last.then_inc(s_mix, 1)

            def conv(c, g):
                if c == 0 and g == 0:
                    eng.wait_ge(s_pool0, 8)
                before = G * c + g - (1 if c == 0 else 0)
                if before > 0:
                    eng.wait_ge(s_u, before)
                eng.wait_ge(s_x2l, G * c + g + 1)
                n = 0
                for k, (hi, lo) in enumerate(((c_hi, c_lo), (y_hi, y_lo))):
                    if k == 1:
                        eng.wait_ge(s_yd[g], 32 * (c + 1))
                    for w, src in ((cw_hi, hi), (cw_hi, lo), (cw_lo, hi)):
                        last = mm(conv_bank(c, g)[:, :], w[:, k, g, :], runs(src, g), start=(n == 0), stop=(n == 5))
                        n += 1
                last.then_inc(s_conv, 1)

            def transpose_u(c, g):
                eng.wait_ge(s_u, G * c + g + 1)
                if c or g:
                    eng.wait_ge(s_utl, G * c + g)
                for n in range(UB):
                    last = eng.transpose(p_ut[:, n * P:(n + 1) * P], u_sb[:, g % 2, n * P:(n + 1) * P], ident[:, :])
                last.then_inc(s_ut, 1)

            def linear(d, slot):
                f, q = slot // 4, slot % 4
                t, j = f // 2, f % 2
                if q == 0:
                    if f == 0:
                        if d == 0:
                            eng.wait_ge(s_wf, 2)
                        eng.wait_ge(s_utl, G * (d + 1))
                    if d or f >= 2:
                        eng.wait_ge(s_res, 4 * d + f - 1)
                if q == 3:
                    with eng.If(inexact != 0):
                        for r in range(R):
                            for u in (u_hi, u_lo):
                                for w in (rest_hi, rest_lo):
                                    mm(p_f[f % 2][:, :], u[:, d % 2, r, t * P:(t + 1) * P],
                                       w[:, :].unsqueeze(1).broadcast_to([P, HALF // P, P]), start=False, stop=False)
                for r in (2 * q, 2 * q + 1):
                    for u in (u_hi, u_lo):
                        last = mm(p_f[f % 2][:, :], u[:, d % 2, r, t * P:(t + 1) * P], w_ffn[:, r, j * HALF:(j + 1) * HALF],
                                  start=(r == 0 and u is u_hi), stop=(r == R - 1 and u is u_lo))
                if q == 3:
                    last.then_inc(s_f, 1)

            eng.wait_ge(s_small, 16 * N_SMALL)
            mm(p_sm[:, 0:B], w0_sb, cond_sb, start=True, stop=True).then_inc(s_pe0, 1)
            eng.wait_ge(s_act0, 1)
            mm(p_sm[:, B:2 * B], w1_sb, h_sb[:, 0, :], start=True, stop=True).then_inc(s_pe0, 1)
            eng.wait_ge(s_act0, 2)
            mm(p_sm[0:B, 128:128 + KE], h_sb[:, 1, :], w2_sb, start=True, stop=True).then_inc(s_pe0, 1)
            eng.wait_ge(s_att, 8)
            eng.wait_ge(s_pool0, 4)
            eng.transpose(p_sm[0:3 * KE, 192:192 + B], att_r[:, :].bitcast(F32), ident[0:B, 0:B]).then_inc(s_pe0, 1)
            eng.wait_ge(s_att, 9)
            mm(p_sm[:, 256:256 + B], mixb_sb, att_t[0:2 * KE, :].bitcast(F32), start=True, stop=True).then_inc(s_pe0, 1)
            for c in range(8):
                if c % 4 == 0:
                    eng.wait_ge(s_mwr, c // 4 + 1)
                if c >= 4:
                    eng.wait_ge(s_mixedc, c - 3)
                mm(p_mixed[c % 4][0:B, :], att_t[:, :], mixw_r[c // 4][:, 512 * (c % 4):512 * (c % 4) + 512],
                   start=True, stop=True).then_inc(s_mixed, 1)

            for k in range(4):
                transpose_x(0, k)
            project(0, 0)
            eng.wait_ge(s_mixb, 2)
            for r in range(R):
                last = mm(p_sm[:, 320:320 + W3], ones[:, :], w3[:, r, :], start=(r == 0), stop=(r == R - 1))
            last.then_inc(s_pe0, 1)
            project(0, 1)
            eng.wait_ge(s_flag, 1)
            inexact = eng.value_load(flag[0:1, 0:1], min_val=0, max_val=1)

            def context_bias():
                eng.wait_ge(s_small2, 16 * N_SMALL2)
                for g in range(G):
                    last = mm(p_conv[:, B * g:B * g + B], ctx_sb[:, g, :], cond_sb, start=True, stop=True)
                last.then_inc(s_pe0, 1)

            for i in range(NI):
                a, c, d = i, i - 2, i - 3
                for slot in range(SLOTS):
                    if 0 <= d < NU:
                        linear(d, slot)
                    (xa, xt_slots, z_slots), (conv_slots, ut_slots) = stage_a(i, slot), stage_c(c)
                    if xa and slot in xt_slots:
                        transpose_x(xa, xt_slots.index(slot))
                    if slot in ut_slots:
                        transpose_u(c, ut_slots.index(slot))
                    if xa and slot in z_slots:
                        project(xa, z_slots.index(slot))
                    if slot in conv_slots:
                        conv(c, conv_slots.index(slot))
                    if a < NU and slot in mix_slots(a):
                        mix(a, mix_slots(a).index(slot))
                        if a == 0 and slot == mix_slots(a)[-1]:
                            context_bias()


def kernel(**inputs):
    import numpy as np
    from concourse import bacc
    from concourse.bass_utils import run_bass_kernel_spmd

    def arr(name):
        return np.asarray(inputs[name])

    conv_w = arr("L0_cond2_weight").reshape(G, CG, CG, TAPS).transpose(2, 0, 3, 1)[:, :, ::-1, :]
    ctx_w = arr("L0_cond2_c_weight").T.reshape(P, G, 1, CG)
    part = np.where(np.arange(P) < 2 * KE, 0, -1).astype(np.float32).reshape(P, 1)
    arrays = {
        "x": arr("x").reshape(B * S, D),
        "cols": np.concatenate([arr("cond_128").T, arr("L0_cond_W0"), arr("L0_cond_W1"), arr("L0_cond_W2"),
                                arr("L0_cond_b0").reshape(P, 1), arr("L0_cond_b1").reshape(P, 1),
                                np.tile(arr("fside_S_0").reshape(G, CG).T, (R, 1)), part], axis=1),
        "row": np.concatenate([arr("L0_ffn_scale").reshape(1), arr("L0_ffn_zero_point").reshape(1), arr("L0_cond_b2"),
                               arr("L0_attn_bk").reshape(DH), arr("L0_attn_bv").reshape(DH)]).reshape(1, NROW),
        "mix_w": np.tile(np.concatenate([arr("L0_cond_bias_k"), arr("L0_cond_bias_k"),
                                         arr("L0_cond_weight").reshape(KE, S, S).transpose(0, 2, 1).reshape(KE, S * S)], axis=1), (3, 1)),
        "wq": arr("L0_attn_Wq").reshape(P, R, DH * NH), "bq": arr("L0_attn_bq").reshape(1, DH * NH),
        "wkv": np.concatenate([arr("L0_attn_Wk").reshape(P, R, DH), arr("L0_attn_Wv").reshape(P, R, DH)], axis=2),
        "conv_w": conv_w.reshape(CG, G, TAPS * CG),
        "ctx_w": np.broadcast_to(ctx_w, (P, G, R, CG)).reshape(P, G, P),
        "packed_t": arr("L0_ffn_packed_weight").T.reshape(P, R, HALF),
        "ffn_bias": arr("L0_ffn_bias").reshape(1, D),
    }
    nc = bacc.Bacc("TRN2", target_bir_lowering=False, num_devices=1)
    args = {}
    for name, a in arrays.items():
        arrays[name] = a = np.ascontiguousarray(a)
        args[name] = nc.dram_tensor(name + "_in", a.shape, mybir.dt.from_np(a.dtype), kind="ExternalInput").ap()
    args["out"] = nc.dram_tensor("out_0", (B * S, D), F32, kind="ExternalOutput").ap()
    block_program(nc, **args)
    r = run_bass_kernel_spmd(nc, [{name + "_in": a for name, a in arrays.items()}], core_ids=[0])
    return r.results[0]["out_0"].reshape(B, S, D)
```
